# Optimizing a Trainium2 kernel written in Bass

```python
import numpy as np
import jax
import jax.numpy as jnp

def _softmax(x, axis=-1):
    return jax.nn.softmax(x, axis=axis)

def _gelu(x):
    return jax.nn.gelu(x, approximate=True)

def _silu(x):
    return jax.nn.silu(x)

def _sigmoid(x):
    return jax.nn.sigmoid(x)

def _layernorm(x, axis=-1, eps=1e-05):
    m = jnp.mean(x, axis=axis, keepdims=True)
    v = jnp.var(x, axis=axis, keepdims=True)
    return (x - m) / jnp.sqrt(v + eps)

def _scatter_add(tgt, idx, src, axis=0):
    return tgt.at[idx].add(src)

def _segment_sum(src, seg, n):
    return jax.ops.segment_sum(src, seg, n)
kernel_name = 'mk_xattn_seq_d2_seqx_r8_b47295'

def setup_inputs(seed: int=0):
    np.random.seed(seed)
    _w = jnp.asarray

    def _rec_inputs():
        import jax
        import jax.numpy as jnp
        _rk = jax.random.key(seed)
        x = -0.0005146 + 1 * jax.random.normal(jax.random.fold_in(_rk, 1), (32, 64, 256), jnp.float32)
        _lenS = 64 - jax.random.randint(jax.random.fold_in(_rk, 7), (32,), 0, max(1, 64 // 4) + 1, jnp.int32)
        _lenS2 = 64 - jax.random.randint(jax.random.fold_in(_rk, 8), (32,), 0, max(1, 64 // 4) + 1, jnp.int32)
        _ctx_2048P = jax.random.normal(jax.random.fold_in(_rk, 11), (32, 16, 256), jnp.float32)
        _ctx_2048c = jax.random.dirichlet(jax.random.fold_in(_rk, 511), 0.3 * jnp.ones((16,), jnp.float32), (32, 64))
        _ctx_2048t = jnp.einsum('bsk,bkd->bsd', _ctx_2048c, _ctx_2048P)
        _ctx_2048t = _ctx_2048t * jax.lax.rsqrt(jnp.mean(jnp.square(_ctx_2048t)) + 1e-12) * 0.953939
        ctx_2048 = -0.000392918 + 0.999932 * (_ctx_2048t + 0.3 * jax.random.normal(jax.random.fold_in(_rk, 611), (32, 64, 256), jnp.float32))
        _validS = jnp.arange(64)[None, :] < _lenS[:, None]
        _validS2 = jnp.arange(64)[None, :] < _lenS2[:, None]
        _causal = jnp.tril(jnp.ones((64, 64), dtype=bool))
        mask_BxS2_ik0 = jnp.where(jnp.broadcast_to(_validS2[:, :], (32, 64)), 0, 1).astype(jnp.int32)
        return (x, ctx_2048, mask_BxS2_ik0)
    x, ctx_2048, mask_BxS2_ik0 = _rec_inputs()

    def _L0_xattn_setup():
        import jax, jax.numpy as jnp
        import numpy as np
        B, P, K, H, NH = (4, 256, 32, 256, 16)
        DH = H // NH
        EPS = 1e-06

        def rmsnorm(x, w):
            var = jnp.mean(jnp.square(x), axis=-1, keepdims=True)
            return x * jax.lax.rsqrt(var + EPS) * w
        key = jax.random.key(seed)
        ks = jax.random.split(key, 12)
        s = 0.02
        return {'x': jax.random.normal(ks[0], (B, P, H), jnp.float32), 'latents': jax.random.normal(ks[1], (B, K, H), jnp.float32), 'attention_mask': jax.random.randint(ks[2], (B, P), 0, 2, jnp.int32), 'q_w': s * jax.random.normal(ks[3], (H, H), jnp.float32), 'q_b': jnp.zeros((H,), jnp.float32), 'kv_w': s * jax.random.normal(ks[4], (H, 2 * H), jnp.float32), 'kv_b': jnp.zeros((2 * H,), jnp.float32), 'out_w': s * jax.random.normal(ks[5], (H, H), jnp.float32), 'out_b': jnp.zeros((H,), jnp.float32), 'postnorm_w': jnp.ones((H,), jnp.float32), 'mlp_w1': s * jax.random.normal(ks[6], (H, 4 * H), jnp.float32), 'mlp_b1': jnp.zeros((4 * H,), jnp.float32), 'mlp_w2': s * jax.random.normal(ks[7], (4 * H, H), jnp.float32), 'mlp_b2': jnp.zeros((H,), jnp.float32)}
    _L0_xattn_all = _L0_xattn_setup()
    _L0_xattn_in = {k: v for k, v in _L0_xattn_all.items() if k in ('q_w', 'q_b', 'kv_w', 'kv_b', 'out_w', 'out_b', 'postnorm_w', 'mlp_w1', 'mlp_b1', 'mlp_w2', 'mlp_b2')}
    del _L0_xattn_all

    def _L1_xattn_setup():
        import jax, jax.numpy as jnp
        import numpy as np
        N_HEAD = 32
        EPS = 1e-05

        def _ln(x, w, b):
            m = jnp.mean(x, axis=-1, keepdims=True)
            v = jnp.mean((x - m) ** 2, axis=-1, keepdims=True)
            return (x - m) * jax.lax.rsqrt(v + EPS) * w + b

        def _forward(x, state, i, ln1_w, ln1_b, ln2_w, ln2_b, maa_x, maa_w, maa_k, maa_v, maa_r, maa_g, maa_w1, maa_w2, time_decay, decay_w1, decay_w2, faaaa, Wr, Wk, Wv, Wg, Wo, gn_w, gn_b, fmaa_k, fmaa_r, fWk, fWr, fWv):
            B, L, C = x.shape
            H = N_HEAD
            S = C // H
            i0 = (2 + S) * i
            xa = _ln(x, ln1_w, ln1_b)
            sx = jnp.concatenate([state[:, i0 + 1][:, None], xa[:, :-1]], axis=1) - xa
            xxx = xa + sx * maa_x
            t = jnp.tanh(xxx @ maa_w1).reshape(B, L, 5, -1)
            m = jnp.einsum('blfd,fdc->blfc', t, maa_w2)
            mw, mk, mv, mr, mg = (m[:, :, j] for j in range(5))
            xw = xa + sx * (maa_w + mw)
            xk = xa + sx * (maa_k + mk)
            xv = xa + sx * (maa_v + mv)
            xr = xa + sx * (maa_r + mr)
            xg = xa + sx * (maa_g + mg)
            w = time_decay + jnp.tanh(xw @ decay_w1) @ decay_w2
            w = jnp.exp(-jnp.exp(w)).reshape(B, L, H, S)
            r = (xr @ Wr.T).reshape(B, L, H, S)
            k = (xk @ Wk.T).reshape(B, L, H, S)
            v = (xv @ Wv.T).reshape(B, L, H, S)
            g = jax.nn.silu(xg @ Wg.T)
            s0 = state[:, i0 + 2:i0 + 2 + S].reshape(B, H, S, S)

            def step(s, inp):
                k_l, v_l, w_l, r_l = inp
                a = k_l[..., :, None] * v_l[..., None, :]
                out = jnp.einsum('bhs,bhst->bht', r_l, faaaa * a + s)
                s_new = a + w_l[..., None] * s
                return (s_new, out)
            seq = tuple((z.transpose(1, 0, 2, 3) for z in (k, v, w, r)))
            _, outs = jax.lax.scan(step, s0, seq)
            y = outs.transpose(1, 0, 2, 3)
            gm = jnp.mean(y, axis=-1, keepdims=True)
            gv = jnp.mean((y - gm) ** 2, axis=-1, keepdims=True)
            y = ((y - gm) * jax.lax.rsqrt(gv + EPS)).reshape(B, L, C) * gn_w + gn_b
            x = x + y * g @ Wo.T
            xc = _ln(x, ln2_w, ln2_b)
            sxc = jnp.concatenate([state[:, i0][:, None], xc[:, :-1]], axis=1) - xc
            xk2 = xc + sxc * fmaa_k
            xr2 = xc + sxc * fmaa_r
            rr = jax.nn.sigmoid(xr2 @ fWr.T)
            kk = jnp.square(jax.nn.relu(xk2 @ fWk.T))
            x = x + rr * (kk @ fWv.T)
            return x
        key = jax.random.key(seed)
        B, L, C, H = (8, 64, 256, N_HEAD)
        S = C // H
        DM, DD = (32, 64)
        ks = jax.random.split(key, 32)
        n = lambda k, shp, s=1.0: jax.random.normal(k, shp, dtype=jnp.float32) * s
        u = lambda k, shp: jax.random.uniform(k, shp, dtype=jnp.float32)
        inp = {'x': n(ks[0], (B, L, C)), 'state': n(ks[1], (B, 2 + S, C), 0.1), 'i': 0, 'ln1_w': jnp.ones((C,), jnp.float32), 'ln1_b': jnp.zeros((C,), jnp.float32), 'ln2_w': jnp.ones((C,), jnp.float32), 'ln2_b': jnp.zeros((C,), jnp.float32), 'maa_x': u(ks[2], (C,)), 'maa_w': u(ks[3], (C,)), 'maa_k': u(ks[4], (C,)), 'maa_v': u(ks[5], (C,)), 'maa_r': u(ks[6], (C,)), 'maa_g': u(ks[7], (C,)), 'maa_w1': n(ks[8], (C, 5 * DM), 0.02), 'maa_w2': n(ks[9], (5, DM, C), 0.02), 'time_decay': n(ks[10], (C,), 0.5), 'decay_w1': n(ks[11], (C, DD), 0.02), 'decay_w2': n(ks[12], (DD, C), 0.02), 'faaaa': n(ks[13], (H, S, 1), 0.1), 'Wr': n(ks[14], (C, C), 0.02), 'Wk': n(ks[15], (C, C), 0.02), 'Wv': n(ks[16], (C, C), 0.02), 'Wg': n(ks[17], (C, C), 0.02), 'Wo': n(ks[18], (C, C), 0.02), 'gn_w': jnp.ones((C,), jnp.float32), 'gn_b': jnp.zeros((C,), jnp.float32), 'fmaa_k': u(ks[19], (C,)), 'fmaa_r': u(ks[20], (C,)), 'fWk': n(ks[21], (C, C), 0.02), 'fWr': n(ks[22], (C, C), 0.02), 'fWv': n(ks[23], (C, C), 0.02)}
        return inp
    _L1_xattn_all = _L1_xattn_setup()
    _L1_xattn_in = {k: v for k, v in _L1_xattn_all.items() if k in ('ln1_w', 'ln1_b', 'ln2_w', 'ln2_b', 'maa_x', 'maa_w', 'maa_k', 'maa_v', 'maa_r', 'maa_g', 'maa_w1', 'maa_w2', 'time_decay', 'decay_w1', 'decay_w2', 'faaaa', 'Wr', 'Wk', 'Wv', 'Wg', 'Wo', 'gn_w', 'gn_b', 'fmaa_k', 'fmaa_r', 'fWk', 'fWr', 'fWv')}
    del _L1_xattn_all
    return {'x': x, 'ctx_2048': ctx_2048, 'mask_BxS2_ik0': mask_BxS2_ik0, 'L0_xattn_q_w': _L0_xattn_in['q_w'], 'L0_xattn_q_b': _L0_xattn_in['q_b'], 'L0_xattn_kv_w': _L0_xattn_in['kv_w'], 'L0_xattn_kv_b': _L0_xattn_in['kv_b'], 'L0_xattn_out_w': _L0_xattn_in['out_w'], 'L0_xattn_out_b': _L0_xattn_in['out_b'], 'L0_xattn_postnorm_w': _L0_xattn_in['postnorm_w'], 'L0_xattn_mlp_w1': _L0_xattn_in['mlp_w1'], 'L0_xattn_mlp_b1': _L0_xattn_in['mlp_b1'], 'L0_xattn_mlp_w2': _L0_xattn_in['mlp_w2'], 'L0_xattn_mlp_b2': _L0_xattn_in['mlp_b2'], 'L1_xattn_ln1_w': _L1_xattn_in['ln1_w'], 'L1_xattn_ln1_b': _L1_xattn_in['ln1_b'], 'L1_xattn_ln2_w': _L1_xattn_in['ln2_w'], 'L1_xattn_ln2_b': _L1_xattn_in['ln2_b'], 'L1_xattn_maa_x': _L1_xattn_in['maa_x'], 'L1_xattn_maa_w': _L1_xattn_in['maa_w'], 'L1_xattn_maa_k': _L1_xattn_in['maa_k'], 'L1_xattn_maa_v': _L1_xattn_in['maa_v'], 'L1_xattn_maa_r': _L1_xattn_in['maa_r'], 'L1_xattn_maa_g': _L1_xattn_in['maa_g'], 'L1_xattn_maa_w1': _L1_xattn_in['maa_w1'], 'L1_xattn_maa_w2': _L1_xattn_in['maa_w2'], 'L1_xattn_time_decay': _L1_xattn_in['time_decay'], 'L1_xattn_decay_w1': _L1_xattn_in['decay_w1'], 'L1_xattn_decay_w2': _L1_xattn_in['decay_w2'], 'L1_xattn_faaaa': _L1_xattn_in['faaaa'], 'L1_xattn_Wr': _L1_xattn_in['Wr'], 'L1_xattn_Wk': _L1_xattn_in['Wk'], 'L1_xattn_Wv': _L1_xattn_in['Wv'], 'L1_xattn_Wg': _L1_xattn_in['Wg'], 'L1_xattn_Wo': _L1_xattn_in['Wo'], 'L1_xattn_gn_w': _L1_xattn_in['gn_w'], 'L1_xattn_gn_b': _L1_xattn_in['gn_b'], 'L1_xattn_fmaa_k': _L1_xattn_in['fmaa_k'], 'L1_xattn_fmaa_r': _L1_xattn_in['fmaa_r'], 'L1_xattn_fWk': _L1_xattn_in['fWk'], 'L1_xattn_fWr': _L1_xattn_in['fWr'], 'L1_xattn_fWv': _L1_xattn_in['fWv']}

def reference(x, ctx_2048, mask_BxS2_ik0, L0_xattn_q_w, L0_xattn_q_b, L0_xattn_kv_w, L0_xattn_kv_b, L0_xattn_out_w, L0_xattn_out_b, L0_xattn_postnorm_w, L0_xattn_mlp_w1, L0_xattn_mlp_b1, L0_xattn_mlp_w2, L0_xattn_mlp_b2, L1_xattn_ln1_w, L1_xattn_ln1_b, L1_xattn_ln2_w, L1_xattn_ln2_b, L1_xattn_maa_x, L1_xattn_maa_w, L1_xattn_maa_k, L1_xattn_maa_v, L1_xattn_maa_r, L1_xattn_maa_g, L1_xattn_maa_w1, L1_xattn_maa_w2, L1_xattn_time_decay, L1_xattn_decay_w1, L1_xattn_decay_w2, L1_xattn_faaaa, L1_xattn_Wr, L1_xattn_Wk, L1_xattn_Wv, L1_xattn_Wg, L1_xattn_Wo, L1_xattn_gn_w, L1_xattn_gn_b, L1_xattn_fmaa_k, L1_xattn_fmaa_r, L1_xattn_fWk, L1_xattn_fWr, L1_xattn_fWv):
    import jax
    import jax.numpy as jnp

    def _L0_xattn_ref(x, latents, attention_mask, q_w, q_b, kv_w, kv_b, out_w, out_b, postnorm_w, mlp_w1, mlp_b1, mlp_w2, mlp_b2):
        import jax, jax.numpy as jnp
        import numpy as np
        B, P, K, H, NH = (4, 256, 32, 256, 16)
        DH = H // NH
        EPS = 1e-06

        def rmsnorm(x, w):
            var = jnp.mean(jnp.square(x), axis=-1, keepdims=True)
            return x * jax.lax.rsqrt(var + EPS) * w
        b, p, _ = x.shape
        k_len = latents.shape[1]
        residual = latents
        h = jnp.concatenate([x, latents], axis=1)
        q = (latents @ q_w + q_b).reshape(b, k_len, NH, DH)
        kv = (h @ kv_w + kv_b).reshape(b, p + k_len, NH, DH, 2)
        kmat, v = (kv[..., 0], kv[..., 1])
        attn = jnp.einsum('bkhd,bnhd->bhkn', q, kmat) / DH
        full_mask = jnp.concatenate([attention_mask.astype(bool), jnp.ones((b, k_len), bool)], axis=-1)
        attn = jnp.where(full_mask[:, None, None, :], attn, -jnp.inf)
        attn = jax.nn.softmax(attn.astype(jnp.float32), axis=-1).astype(q.dtype)
        attn_out = jnp.einsum('bhkn,bnhd->bkhd', attn, v).reshape(b, k_len, H)
        attn_out = attn_out @ out_w + out_b + residual
        out = rmsnorm(attn_out, postnorm_w)
        out = jax.nn.gelu(out @ mlp_w1 + mlp_b1) @ mlp_w2 + mlp_b2
        return out + residual

    def _L1_xattn_ref(x, state, i, ln1_w, ln1_b, ln2_w, ln2_b, maa_x, maa_w, maa_k, maa_v, maa_r, maa_g, maa_w1, maa_w2, time_decay, decay_w1, decay_w2, faaaa, Wr, Wk, Wv, Wg, Wo, gn_w, gn_b, fmaa_k, fmaa_r, fWk, fWr, fWv):
        import jax, jax.numpy as jnp
        import numpy as np
        N_HEAD = 32
        EPS = 1e-05

        def _ln(x, w, b):
            m = jnp.mean(x, axis=-1, keepdims=True)
            v = jnp.mean((x - m) ** 2, axis=-1, keepdims=True)
            return (x - m) * jax.lax.rsqrt(v + EPS) * w + b

        def _forward(x, state, i, ln1_w, ln1_b, ln2_w, ln2_b, maa_x, maa_w, maa_k, maa_v, maa_r, maa_g, maa_w1, maa_w2, time_decay, decay_w1, decay_w2, faaaa, Wr, Wk, Wv, Wg, Wo, gn_w, gn_b, fmaa_k, fmaa_r, fWk, fWr, fWv):
            B, L, C = x.shape
            H = N_HEAD
            S = C // H
            i0 = (2 + S) * i
            xa = _ln(x, ln1_w, ln1_b)
            sx = jnp.concatenate([state[:, i0 + 1][:, None], xa[:, :-1]], axis=1) - xa
            xxx = xa + sx * maa_x
            t = jnp.tanh(xxx @ maa_w1).reshape(B, L, 5, -1)
            m = jnp.einsum('blfd,fdc->blfc', t, maa_w2)
            mw, mk, mv, mr, mg = (m[:, :, j] for j in range(5))
            xw = xa + sx * (maa_w + mw)
            xk = xa + sx * (maa_k + mk)
            xv = xa + sx * (maa_v + mv)
            xr = xa + sx * (maa_r + mr)
            xg = xa + sx * (maa_g + mg)
            w = time_decay + jnp.tanh(xw @ decay_w1) @ decay_w2
            w = jnp.exp(-jnp.exp(w)).reshape(B, L, H, S)
            r = (xr @ Wr.T).reshape(B, L, H, S)
            k = (xk @ Wk.T).reshape(B, L, H, S)
            v = (xv @ Wv.T).reshape(B, L, H, S)
            g = jax.nn.silu(xg @ Wg.T)
            s0 = state[:, i0 + 2:i0 + 2 + S].reshape(B, H, S, S)

            def step(s, inp):
                k_l, v_l, w_l, r_l = inp
                a = k_l[..., :, None] * v_l[..., None, :]
                out = jnp.einsum('bhs,bhst->bht', r_l, faaaa * a + s)
                s_new = a + w_l[..., None] * s
                return (s_new, out)
            seq = tuple((z.transpose(1, 0, 2, 3) for z in (k, v, w, r)))
            _, outs = jax.lax.scan(step, s0, seq)
            y = outs.transpose(1, 0, 2, 3)
            gm = jnp.mean(y, axis=-1, keepdims=True)
            gv = jnp.mean((y - gm) ** 2, axis=-1, keepdims=True)
            y = ((y - gm) * jax.lax.rsqrt(gv + EPS)).reshape(B, L, C) * gn_w + gn_b
            x = x + y * g @ Wo.T
            xc = _ln(x, ln2_w, ln2_b)
            sxc = jnp.concatenate([state[:, i0][:, None], xc[:, :-1]], axis=1) - xc
            xk2 = xc + sxc * fmaa_k
            xr2 = xc + sxc * fmaa_r
            rr = jax.nn.sigmoid(xr2 @ fWr.T)
            kk = jnp.square(jax.nn.relu(xk2 @ fWk.T))
            x = x + rr * (kk @ fWv.T)
            return x
        return _forward(x, state, i, ln1_w, ln1_b, ln2_w, ln2_b, maa_x, maa_w, maa_k, maa_v, maa_r, maa_g, maa_w1, maa_w2, time_decay, decay_w1, decay_w2, faaaa, Wr, Wk, Wv, Wg, Wo, gn_w, gn_b, fmaa_k, fmaa_r, fWk, fWr, fWv)
    x = _L0_xattn_ref(ctx_2048, x, mask_BxS2_ik0, L0_xattn_q_w, L0_xattn_q_b, L0_xattn_kv_w, L0_xattn_kv_b, L0_xattn_out_w, L0_xattn_out_b, L0_xattn_postnorm_w, L0_xattn_mlp_w1, L0_xattn_mlp_b1, L0_xattn_mlp_w2, L0_xattn_mlp_b2)
    x = _L1_xattn_ref(x, ctx_2048, 0, L1_xattn_ln1_w, L1_xattn_ln1_b, L1_xattn_ln2_w, L1_xattn_ln2_b, L1_xattn_maa_x, L1_xattn_maa_w, L1_xattn_maa_k, L1_xattn_maa_v, L1_xattn_maa_r, L1_xattn_maa_g, L1_xattn_maa_w1, L1_xattn_maa_w2, L1_xattn_time_decay, L1_xattn_decay_w1, L1_xattn_decay_w2, L1_xattn_faaaa, L1_xattn_Wr, L1_xattn_Wk, L1_xattn_Wv, L1_xattn_Wg, L1_xattn_Wo, L1_xattn_gn_w, L1_xattn_gn_b, L1_xattn_fmaa_k, L1_xattn_fmaa_r, L1_xattn_fWk, L1_xattn_fWr, L1_xattn_fWv)
    return x

_drawn_inputs = setup_inputs


def setup_inputs(seed=0):
    import zlib

    import numpy as np

    out = dict(_drawn_inputs(seed))
    spreads = {'L0_xattn_q_b': (0.0, 0.8),
     'L0_xattn_kv_b': (0.0, 0.8),
     'L0_xattn_out_b': (0.0, 2.0),
     'L0_xattn_postnorm_w': (1.0, 0.6),
     'L0_xattn_mlp_b1': (0.0, 0.1),
     'L0_xattn_mlp_b2': (0.0, 0.1),
     'L1_xattn_ln1_w': (1.0, 0.6),
     'L1_xattn_ln1_b': (0.0, 0.566),
     'L1_xattn_ln2_w': (1.0, 0.6),
     'L1_xattn_ln2_b': (0.0, 0.8),
     'L1_xattn_gn_w': (1.0, 0.6),
     'L1_xattn_gn_b': (0.0, 0.8)}
    factors = {'ctx_2048': 4.721,
     'L0_xattn_q_w': 8.0,
     'L0_xattn_kv_w': 8.0,
     'L0_xattn_out_w': 8.0,
     'L1_xattn_maa_x': 8.0,
     'L1_xattn_maa_w': 8.0,
     'L1_xattn_maa_w1': 8.0,
     'L1_xattn_maa_w2': 8.0,
     'L1_xattn_time_decay': 3.519,
     'L1_xattn_decay_w1': 8.0,
     'L1_xattn_decay_w2': 8.0,
     'L1_xattn_faaaa': 7.571,
     'L1_xattn_fmaa_k': 7.35,
     'L1_xattn_fmaa_r': 8.0,
     'L1_xattn_fWk': 4.144,
     'L1_xattn_fWr': 8.0,
     'L1_xattn_fWv': 3.799}
    for name, (base, spread) in spreads.items():
        noise = np.random.default_rng([zlib.crc32(name.encode()), seed]).standard_normal(out[name].shape)
        drawn = base * np.exp(spread * noise) if base else spread * noise
        out[name] = jnp.asarray(drawn.astype(out[name].dtype))
    for name, factor in factors.items():
        out[name] = (out[name] * factor).astype(out[name].dtype)
    return out
```

```python
from contextlib import ExitStack

import numpy as np

import concourse.bass as bass
from concourse import mybir

B, L, C = 32, 64, 256
KEYS = 2 * L
NH0, DH = 16, 16
NH1, S = 32, 8
F = 4 * C
MAA = 5
DM, DD = 32, 64
P = 128
H = C // P
GB = 4
T = GB * L
TT = T // P
GROUPS = B // GB
R = 4
NS = (GB // 2) * R
FC = F // P
EPS0, EPS1 = 1e-6, 1e-5
MASKED = -1e30

BANK_USES = [
    ["q", "v1", "s1", "s3", "s5", "s7", "out", "m2"],
    ["k0", "s0", "s2", "s4", "s6", "norm", "m3"],
    ["k1", "p0", "p2", "p4", "p5", "p7", "m0", "mlp"],
    ["v0", "p1", "p3", "o0", "p6", "o1", "m1"],
    ["xa", "mix2", "decay2", "g", "vr0", "vr3", "vr6", "rstd", "fr"],
    ["maa", "mix3", "k", "vc", "vr1", "vr4", "vr7", "wo", "fv"],
    ["mix0", "mix4", "v", "bonus", "vr2", "vr5", "var", "fk"],
    ["mix1", "decay1", "r", "y", "xc"],
]
BANK_OF = {use: (b, k, len(uses)) for b, uses in enumerate(BANK_USES) for k, use in enumerate(uses)}
SETUP = 7


def build(nc, io):
    f32, bf16, i32 = mybir.dt.float32, mybir.dt.bfloat16, mybir.dt.int32
    ALU, ACT, AX = mybir.AluOpType, mybir.ActivationFunctionType, mybir.AxisListType
    mult, add, sub, amax = ALU.mult, ALU.add, ALU.subtract, ALU.max

    with ExitStack() as ctx:
        def sb(name, shape, dt=f32):
            return ctx.enter_context(nc.sbuf_tensor(name, shape, dt))

        def sem(name):
            return ctx.enter_context(nc.semaphore(name))

        q_w, k_w, v_w, out_w = (sb(n, [P, H, C]) for n in ("q_w", "k_w", "v_w", "out_w"))
        w1 = sb("w1", [P, H, F])
        w2 = sb("w2", [P, FC, C])
        maa_w1 = sb("maa_w1", [P, H, MAA * DM])
        maa_w2 = sb("maa_w2", [P, C])
        maa_w2g = sb("maa_w2g", [DM, C])
        decay_w1 = sb("decay_w1", [P, H, DD])
        decay_w2 = sb("decay_w2", [DD, C])
        wr, wk, wv, wg, wo, fwk, fwr, fwv = (
            sb(n, [P, H, C]) for n in ("wr", "wk", "wv", "wg", "wo", "fwk", "fwr", "fwv"))
        cols = sb("cols", [P, 19, H])
        (QB, KB, POST, LN1W, LN1B, LN2W, LN2B, MAAX, MAA0, TD, U, GNW, GNB, FMK, FMR) = (
            0, 1, 2, 3, 4, 5, 6, 7, 8, 13, 14, 15, 16, 17, 18)
        b1 = sb("b1", [P, FC])
        rows = sb("rows", [P, 3, C])
        VB, OB, B2 = 0, 1, 2
        ident = sb("ident", [P, P])
        block = sb("block", [P, P])
        centre = sb("centre", [P, P])
        mean16 = sb("mean16", [P, P // S])
        rep = sb("rep", [P, S, P])
        fold = sb("fold", [P, S, P])
        parity = sb("parity", [P, 2])
        q_bias = sb("q_bias", [P, H, 2])
        gn_half = sb("gn_half", [P, 2, H])
        power = sb("power", [P, TT * NH1])
        ones = sb("ones", [P, P], bf16)
        mask_i = sb("mask_i", [P, GB, L], i32)
        mask = sb("mask", [P, GB, KEYS], bf16)
        s0 = sb("s0", [P, GROUPS, S, H * GB])
        edge = sb("edge", [P, GROUPS, 2, H * GB])

        kv = sb("kv", [P, S, H * GB, L])
        h_T = sb("h_T", [P, H, GB, KEYS])
        x_tok = sb("x_tok", [P, TT, C])
        x_ob, x_b2 = sb("x_ob", [P, TT, C]), sb("x_b2", [P, TT, C])
        q_T = sb("q_T", [P, H, GB, 2, L])
        k_T = sb("k_T", [P, H, GB, KEYS])
        v_z = sb("v_z", [P, GB, H * R, 4, DH])
        nmax = sb("nmax", [P, NS, 4])
        den = sb("den", [P, NS, 4])
        rden = sb("rden", [P, NS, 4])
        prob = sb("prob", [P, 4, 4, KEYS])
        prob_T = sb("prob_T", [P, GB // 2, R, 4, P])
        att_T = sb("att_T", [P, H, T])
        res = sb("res", [P, TT, C])
        ss, ssm, rms = sb("ss", [P, TT]), sb("ssm", [P, TT]), sb("rms", [P, TT])
        nrm = sb("nrm", [P, TT, C])
        n_T = sb("n_T", [P, H, T])
        hid = sb("hid", [P, FC, T])
        x1 = sb("x1", [P, TT, C])
        x2 = sb("x2", [P, TT, C])
        stats = sb("stats", [P, 2, TT, 6])
        carrier = sb("carrier", [1, 1])
        mv = sb("mv", [P, 2, TT, 2])
        vare, rstd = sb("vare", [P, 2, TT]), sb("rstd_ln", [P, 2, TT])
        xh = sb("xh", [P, TT, C])
        xa = sb("xa", [P, H, GB, L + 1])
        g_wide = xh
        sx = sb("sx", [P, H, GB, L])
        xx = sb("xx", [P, H, T])
        th, thg = sb("th", [P, T]), sb("thg", [DM, T])
        mixed = sb("mixed", [P, MAA, H, T])
        d1 = sb("d1", [DD, T])
        w_sh = sb("w_sh", [P, H, GB, L])
        k1, v1, r1 = sb("k1", [P, H, GB, L]), sb("v1", [P, H, GB, L]), sb("r1", [P, H, GB, L])
        gate = sb("gate", [P, H, T])
        ew = gate[:, :, :].rearrange("p h (b l) -> p h b l", l=L)
        v_c = sb("v_c", [P, H * T])
        ruk, bonus = sb("ruk", [P, H, T]), sb("bonus", [P, H * T])
        NR = 3
        state = sb("state", [P, NR, H * T])
        rs = sb("rs", [P, NR, H * T])
        yc = sb("yc", [P, H, T])
        sq = ruk
        gv, g_rstd = sb("gv", [P, TT * NH1]), sb("g_rstd", [P, TT * NH1])
        z = sb("z", [P, H, T])
        xk2, xr2 = xx, sb("xr2", [P, H, T])
        kk = z
        tr, o = xh, sb("o", [P, TT, C])

        bank = [ctx.enter_context(nc.psum_tensor(f"bank{b}", [P, 512], f32)) for b in range(8)]
        bank_full = [sem(f"bank_full{b}") for b in range(8)]
        bank_free = [sem(f"bank_free{b}") for b in range(8)]

        def psum(use):
            return bank[BANK_OF[use][0]]

        def first(g):
            return isinstance(g, int) and g == 0

        def full(eng, use, g):
            b, k, n = BANK_OF[use]
            eng.wait_ge(bank_full[b], g * n + (k + 1))

        def room(eng, use, g):
            b, k, n = BANK_OF[use]
            if not first(g) or k:
                eng.wait_ge(bank_free[b], g * n + k)

        def taken(eng, use, g):
            b, k, n = BANK_OF[use]
            eng.wait_ge(bank_free[b], g * n + (k + 1))

        def filled(ins, use):
            ins.then_inc(bank_full[BANK_OF[use][0]], 1)

        def freed(ins, use):
            ins.then_inc(bank_free[BANK_OF[use][0]], 1)

        l0_w, l1_w, small_w = sem("l0_w"), sem("l1_w"), sem("small_w")
        mask_in, mask_done = sem("mask_in"), sem("mask_done")
        h_in, x_in, out_done = sem("h_in"), sem("x_in"), sem("out_done")
        setup = sem("setup")
        nmax_done = sem("nmax_done")
        rden_done = sem("rden_done")
        prob_done = sem("prob_done")
        xob_done, xb2_done = sem("xob_done"), sem("xb2_done")
        ss_done, ssm_done, rms_done, nrm_done = sem("ss_done"), sem("ssm_done"), sem("rms_done"), sem("nrm_done")
        stat_done, mv_done = sem("stat_done"), sem("mv_done")
        vare_done, rstd_done, xh_done = sem("vare_done"), sem("rstd_done"), sem("xh_done")
        edge_done, sx_done, xx_done = sem("edge_done"), sem("sx_done"), sem("xx_done")
        mixed_done = sem("mixed_done")
        w_done, tg_done, ruk_done = sem("w_done"), sem("tg_done"), sem("ruk_done")
        s0_done, state_done, rs_done = sem("s0_done"), sem("state_done"), sem("rs_done")
        sq_done, grstd_done, gwide_done, z2_done, z_done = sem("sq_done"), sem("grstd_done"), sem("gwide_done"), sem("z2_done"), sem("z_done")
        xkr_done, kk_done, o_done = sem("xkr_done"), sem("kk_done"), sem("o_done")

        def seqs(ap):
            return ap.rearrange("p (a l) -> p a l", l=L)

        blk = ctx.enter_context(nc.Block())

        L0_LOADS = [(q_w, "q_w"), (k_w, "k_w"), (v_w, "v_w")]
        L0_LATER = [(ident, "ident"), (out_w, "out_w"), (w1, "w1"), (w2, "w2")]
        SMALL = [(b1, "b1"), (rows, "rows"), (cols, "cols"), (parity, "parity")]
        L1_LOADS = [(maa_w1, "maa_w1"), (maa_w2, "maa_w2"), (maa_w2g, "maa_w2g"), (decay_w1, "decay_w1"),
                    (decay_w2, "decay_w2"), (wr, "wr"), (wk, "wk"), (wv, "wv"), (wg, "wg"), (wo, "wo"),
                    (fwk, "fwk"), (fwr, "fwr"), (fwv, "fwv"), (block, "block"), (centre, "centre"),
                    (mean16, "mean16"), (rep, "rep"), (fold, "fold"), (s0, "s0"), (edge, "edge")]

        @blk.sync
        def _(sp):
            def load_h(g):
                if not first(g):
                    full(sp, "v1", g - 1)
                sp.dma_start(h_T[:, :, :, :], io["h_T"][bass.ds(g, 1), :, :].rearrange(
                    "g p (h b k) -> p (g h) b k", h=H, b=GB)).then_inc(h_in, 16)

            def load_mask(g):
                if not first(g):
                    sp.wait_ge(mask_done, g)
                sp.dma_start(mask_i[:, :, :], io["mask"][:, bass.ds(g * GB, GB), :].broadcast_to([P, GB, L])).then_inc(mask_in, 16)

            def load_x(g):
                if not first(g):
                    sp.wait_ge(xob_done, g)
                    sp.wait_ge(xb2_done, g)
                sp.dma_start(x_tok[:, :, :], io["x"][bass.ds(g * T, T), :].rearrange(
                    "(t p) c -> p t c", p=P)).then_inc(x_in, 16)

            def store(g):
                sp.wait_ge(o_done, g + 1)
                sp.dma_start(io["out"][bass.ds(g * T, T), :].rearrange("(t p) c -> p t c", p=P),
                             o[:, :, :]).then_inc(out_done, 16)

            for dst, name in L0_LOADS:
                sp.dma_start(dst[:, :, :], io[name]).then_inc(l0_w, 16)
            load_h(0)
            load_mask(0)
            load_x(0)
            for dst, name in L0_LATER:
                sp.dma_start(dst[:], io[name]).then_inc(l0_w, 16)
            load_h(1)
            load_mask(1)
            load_x(1)
            store(0)
            with sp.Fori(2, GROUPS) as i:
                load_h(i)
                load_mask(i)
                load_x(i)
                store(i - 1)
            store(GROUPS - 1)
            sp.wait_ge(out_done, 16 * GROUPS)

        @blk.tensor
        def _(pe):
            mm = nc.tensor.matmul

            def project_T(use, w, x, g):
                room(pe, use, g)
                for m in range(H):
                    for k in range(H):
                        last = mm(psum(use)[:, m * T:(m + 1) * T], w[:, k, m * P:(m + 1) * P], x[:, k, :],
                                  start=k == 0, stop=k == H - 1)
                filled(last, use)

            def project_tok(use, x, w, g, chunks=H):
                room(pe, use, g)
                for t in range(TT):
                    for k in range(chunks):
                        last = mm(psum(use)[:, t * C:(t + 1) * C], x[:, k, t * P:(t + 1) * P], w[:, k, :],
                                  start=k == 0, stop=k == chunks - 1)
                filled(last, use)

            def turn(use, x, g):
                room(pe, use, g)
                for t in range(TT):
                    for h in range(H):
                        last = nc.tensor.transpose(psum(use)[:, h * T + t * P:h * T + (t + 1) * P],
                                                   x[:, t, h * P:(h + 1) * P], ident[:, :])
                filled(last, use)

            def q_proj(g):
                pe.wait_ge(h_in, g * 16 + 16)
                room(pe, "q", g)
                for m in range(H):
                    for k in range(H):
                        last = mm(psum("q")[:, m * T:(m + 1) * T], q_w[:, k, m * P:(m + 1) * P],
                                  h_T[:, k, :, L:KEYS], start=k == 0, stop=k == H - 1)
                filled(last, "q")

            def k_proj(g):
                for m in range(H):
                    room(pe, f"k{m}", g)
                    for k in range(H):
                        last = mm(psum(f"k{m}")[:, :], k_w[:, k, m * P:(m + 1) * P], h_T[:, k, :, :],
                                  start=k == 0, stop=k == H - 1)
                    filled(last, f"k{m}")

            def v_proj(g):
                for n in range(2):
                    room(pe, f"v{n}", g)
                    for j in range(2):
                        for k in range(H):
                            last = mm(psum(f"v{n}")[:, j * C:(j + 1) * C], h_T[:, k, 2 * n + j, :], v_w[:, k, :],
                                      start=k == 0, stop=k == H - 1)
                    filled(last, f"v{n}")

            def scores(n, g):
                bp, r = n // R, n % R
                if n == 0:
                    taken(pe, "q", g)
                    taken(pe, "k0", g)
                    taken(pe, "k1", g)
                    pe.wait_ge(mask_done, g + 1)
                room(pe, f"s{n}", g)
                out = psum(f"s{n}")
                for j in range(4):
                    b, h = 2 * bp + j // 2, j % 2
                    mm(out[:, j * P:(j + 1) * P], ones[32 * r:32 * r + 1, :], mask[32 * r:32 * r + 1, b, :],
                       start=True, stop=False)
                    last = mm(out[:, j * P:(j + 1) * P], q_T[32 * r:32 * r + 32, h, b, :, :],
                              k_T[32 * r:32 * r + 32, h, b, :], start=False, stop=True)
                filled(last, f"s{n}")

            def turn_probs(n, g):
                pe.wait_ge(prob_done, g * NS + n + 1)
                room(pe, f"p{n}", g)
                for j in range(4):
                    last = nc.tensor.transpose(psum(f"p{n}")[:, j * P:(j + 1) * P], prob[:, n % 4, j, :], ident[:, :])
                filled(last, f"p{n}")

            def attend(bp, g):
                taken(pe, f"p{R * bp + 2}", g)
                taken(pe, f"p{R * bp + 3}", g)
                if bp:
                    taken(pe, "v1", g)
                room(pe, f"o{bp}", g)
                for j in range(4):
                    b, h = 2 * bp + j // 2, j % 2
                    c = h * P + (j // 2) * L
                    for par in range(2):
                        for r in range(R):
                            last = mm(psum(f"o{bp}")[32 * r:32 * r + 32, c:c + L],
                                      v_z[:, b, h * R + r, 2 * par:2 * par + 2, :],
                                      prob_T[:, bp, r, j, par * L:(par + 1) * L], start=par == 0, stop=par == 1)
                filled(last, f"o{bp}")

            def out_proj(g):
                taken(pe, "o1", g)
                project_tok("out", att_T, out_w, g)

            def turn_norm(g):
                pe.wait_ge(nrm_done, g + 1)
                turn("norm", nrm, g)

            def mlp_up(n, g):
                if n == 0:
                    taken(pe, "norm", g)
                room(pe, f"m{n}", g)
                for j in range(2):
                    c = (2 * n + j) * P
                    for k in range(H):
                        last = mm(psum(f"m{n}")[:, j * T:(j + 1) * T], w1[:, k, c:c + P], n_T[:, k, :],
                                  start=k == 0, stop=k == H - 1)
                filled(last, f"m{n}")

            def mlp_down(g):
                for n in range(FC // 2):
                    taken(pe, f"m{n}", g)
                project_tok("mlp", hid, w2, g, FC)

            def turn_xa(g):
                pe.wait_ge(xh_done, g * 2 + 1)
                turn("xa", xh, g)

            def maa(g):
                pe.wait_ge(xx_done, g + 1)
                room(pe, "maa", g)
                for k in range(H):
                    mm(psum("maa")[:, 0:T], maa_w1[:, k, 0:P], xx[:, k, :], start=k == 0, stop=k == H - 1)
                for k in range(H):
                    last = mm(psum("maa")[0:DM, T:2 * T], maa_w1[:, k, P:P + DM], xx[:, k, :],
                              start=k == 0, stop=k == H - 1)
                filled(last, "maa")

            def mix(f, g):
                if f == 0:
                    taken(pe, "maa", g)
                room(pe, f"mix{f}", g)
                for h in range(H):
                    if f < 4:
                        w, x = maa_w2[32 * f:32 * f + 32, h * P:(h + 1) * P], th[32 * f:32 * f + 32, :]
                    else:
                        w, x = maa_w2g[:, h * P:(h + 1) * P], thg[:, :]
                    last = mm(psum(f"mix{f}")[:, h * T:(h + 1) * T], w, x, start=True, stop=True)
                filled(last, f"mix{f}")

            def decay1(g):
                pe.wait_ge(mixed_done, g * MAA + 1)
                room(pe, "decay1", g)
                for k in range(H):
                    last = mm(psum("decay1")[0:DD, 0:T], decay_w1[:, k, :], mixed[:, 0, k, :],
                              start=k == 0, stop=k == H - 1)
                filled(last, "decay1")

            def decay2(g):
                taken(pe, "decay1", g)
                room(pe, "decay2", g)
                for h in range(H):
                    last = mm(psum("decay2")[:, h * T:(h + 1) * T], decay_w2[:, h * P:(h + 1) * P], d1[:, :],
                              start=True, stop=True)
                filled(last, "decay2")

            def proj(use, f, w, g):
                pe.wait_ge(mixed_done, g * MAA + f + 1)
                project_T(use, w, mixed[:, f, :, :], g)

            def v_centred(g):
                taken(pe, "v", g)
                room(pe, "vc", g)
                filled(mm(psum("vc")[:, :], centre[:, :], v1[:, :, :, :], start=True, stop=True), "vc")

            def bonus_sum(g):
                pe.wait_ge(ruk_done, g + 1)
                room(pe, "bonus", g)
                filled(mm(psum("bonus")[:, :], block[:, :], ruk[:, :, :], start=True, stop=True), "bonus")

            def v_rep(t, g):
                room(pe, f"vr{t}", g)
                filled(mm(psum(f"vr{t}")[:, :], rep[:, t, :], v1[:, :, :, :], start=True, stop=True), f"vr{t}")

            def y_sum(t, g):
                pe.wait_ge(rs_done, g * S + t + 1)
                if t == 0:
                    room(pe, "y", g)
                last = mm(psum("y")[:, :], fold[:, t, :], rs[:, t % NR, :], start=t == 0, stop=t == S - 1)
                if t == S - 1:
                    filled(last, "y")

            def variance(g):
                pe.wait_ge(sq_done, g + 1)
                room(pe, "var", g)
                n = P // S
                for t in range(TT):
                    for h in range(H):
                        c = (t * H + h) * n
                        last = mm(psum("var")[:, c:c + n], sq[:, h, t * P:(t + 1) * P], mean16[:, :],
                                  start=True, stop=True)
                filled(last, "var")

            def turn_rstd(g):
                pe.wait_ge(gwide_done, g + 1)
                room(pe, "rstd", g)
                for t in range(TT):
                    for h in range(H):
                        last = nc.tensor.transpose(psum("rstd")[:, h * T + t * P:h * T + (t + 1) * P],
                                                   g_wide[:, t, h * P:(h + 1) * P], ident[:, :])
                filled(last, "rstd")

            def w_out(g):
                pe.wait_ge(z_done, g + 1)
                project_tok("wo", z, wo, g)

            def turn_xc(g):
                pe.wait_ge(xh_done, g * 2 + 2)
                turn("xc", xh, g)

            def ffn(g):
                pe.wait_ge(xkr_done, g + 1)
                project_T("fk", fwk, xk2, g)
                project_tok("fr", xr2, fwr, g)
                pe.wait_ge(kk_done, g + 1)
                project_tok("fv", kk, fwv, g)

            def both(g0, g1):
                a, b = g0 is not None, g1 is not None
                if a: q_proj(g0); k_proj(g0)
                if b: turn_xa(g1)
                if a: v_proj(g0)
                if b: maa(g1)
                for n in range(NS + 3):
                    if a and n < NS: scores(n, g0)
                    if b and n < MAA: mix(n, g1)
                    if b and n == 5: proj("k", 1, wk, g1)
                    if b and n == 4: decay1(g1)
                    if b and n == 6: decay2(g1); proj("v", 2, wv, g1)
                    if b and n == 7: proj("r", 3, wr, g1)
                    if b and n == 8: proj("g", 4, wg, g1); v_centred(g1)
                    if a and n >= 3: turn_probs(n - 3, g0)
                    if a and n == R + 3: attend(0, g0)
                if b: bonus_sum(g1); v_rep(0, g1); v_rep(1, g1)
                if a: attend(1, g0)
                if b: v_rep(2, g1)
                if a: out_proj(g0)
                for t in range(S):
                    if b:
                        y_sum(t, g1)
                        if t + 3 < S: v_rep(t + 3, g1)
                    if a and t == 2: turn_norm(g0)
                    if a and t >= 4: mlp_up(t - 4, g0)
                if b: variance(g1)
                if a: mlp_down(g0)
                if b: turn_rstd(g1); w_out(g1); turn_xc(g1); ffn(g1)

            pe.wait_ge(l0_w, 16 * (len(L0_LOADS) + len(L0_LATER)))
            pe.wait_ge(setup, SETUP)
            both(0, None)
            pe.wait_ge(l1_w, 16 * len(L1_LOADS))
            both(1, 0)
            with pe.Fori(2, GROUPS) as i:
                both(i, i - 1)
            both(None, GROUPS - 1)

        @blk.scalar
        def _(act):
            fn = nc.scalar.activation

            def q_out(g):
                full(act, "q", g)
                for h in range(H):
                    for par in range(2):
                        last = fn(q_T[:, h, :, par, :], seqs(psum("q")[:, h * T:(h + 1) * T]), ACT.Identity,
                                  bias=q_bias[:, h, par:par + 1], scale=parity[:, par:par + 1])
                freed(last, "q")

            def k_out(g):
                for m in range(H):
                    full(act, f"k{m}", g)
                    freed(fn(k_T[:, m, :, :], psum(f"k{m}")[:, :].rearrange("p (b k) -> p b k", b=GB),
                             ACT.Identity, bias=cols[:, KB, m:m + 1]), f"k{m}")

            def exps(n, g):
                act.wait_ge(nmax_done, g * NS + n + 1)
                for j in range(4):
                    last = fn(prob[:, n % 4, j, :], psum(f"s{n}")[:, j * P:(j + 1) * P], ACT.Exp,
                              bias=nmax[:, n, j:j + 1], accum_out=den[:, n, j:j + 1])
                freed(last, f"s{n}")

            def probs_T(n, g):
                full(act, f"p{n}", g)
                freed(fn(prob_T[:, n // R, n % R, :, :], psum(f"p{n}")[:, :].rearrange("p (j q) -> p j q", j=4),
                         ACT.Copy), f"p{n}")

            def squares(g):
                taken(act, "out", g)
                for t in range(TT):
                    last = fn(nrm[:, t, :], res[:, t, :], ACT.Square, accum_out=ss[:, t:t + 1])
                last.then_inc(ss_done, 1)

            def norm_T(g):
                full(act, "norm", g)
                for h in range(H):
                    last = fn(n_T[:, h, :], psum("norm")[:, h * T:(h + 1) * T], ACT.Identity,
                              scale=cols[:, POST, h:h + 1])
                freed(last, "norm")

            def gelu(n, g):
                full(act, f"m{n}", g)
                for j in range(2):
                    c = 2 * n + j
                    last = fn(hid[:, c, :], psum(f"m{n}")[:, j * T:(j + 1) * T], ACT.Gelu_apprx_tanh,
                              bias=b1[:, c:c + 1])
                freed(last, f"m{n}")

            def maa_tanh(g):
                full(act, "maa", g)
                fn(th[:, :], psum("maa")[:, 0:T], ACT.Tanh)
                freed(fn(thg[:, :], psum("maa")[0:DM, T:2 * T], ACT.Tanh), "maa")

            def decay_tanh(g):
                full(act, "decay1", g)
                freed(fn(d1[:, :], psum("decay1")[0:DD, 0:T], ACT.Tanh), "decay1")

            def decays(g):
                full(act, "decay2", g)
                for h in range(H):
                    last = fn(ew[:, h, :, :], seqs(psum("decay2")[:, h * T:(h + 1) * T]), ACT.Exp,
                              bias=cols[:, TD, h:h + 1])
                freed(last, "decay2")
                taken(act, "decay2", g)
                fn(w_sh[:, :, :, 1:L].rearrange("p h b l -> p (h b) l"),
                   ew[:, :, :, 0:L - 1].rearrange("p h b l -> p (h b) l"), ACT.Exp, scale=-1.0).then_inc(w_done, 1)

            def keep(use, dst, g):
                full(act, use, g)
                freed(fn(dst, psum(use)[:, :], ACT.Copy), use)

            def gate_tanh(g):
                full(act, "g", g)
                act.wait_ge(w_done, g + 1)
                fn(gate[:, :, :], psum("g")[:, :], ACT.Tanh, scale=0.5).then_inc(tg_done, 1)

            def y_square(g):
                taken(act, "y", g)
                fn(sq[:, :, :], yc[:, :, :], ACT.Square).then_inc(sq_done, 1)

            def relu_square(g):
                full(act, "fk", g)
                freed(fn(kk[:, :, :], psum("fk")[:, :], ACT.Relu), "fk")
                taken(act, "fk", g)
                fn(kk[:, :, :], kk[:, :, :], ACT.Square).then_inc(kk_done, 1)

            def recept_tanh(g):
                full(act, "fr", g)
                freed(fn(tr[:, :, :], psum("fr")[:, :], ACT.Tanh, scale=0.5), "fr")

            def both(g0, g1):
                a, b = g0 is not None, g1 is not None
                if a: q_out(g0); k_out(g0)
                if b: maa_tanh(g1)
                for n in range(NS + 3):
                    if a and n < NS: exps(n, g0)
                    if b and n == 4: decay_tanh(g1)
                    if b and n == 5: keep("k", k1[:, :, :, :], g1)
                    if b and n == 6: decays(g1); keep("v", v1[:, :, :, :], g1)
                    if b and n == 7: keep("r", r1[:, :, :, :], g1)
                    if b and n == 8: gate_tanh(g1); keep("vc", v_c[:, :], g1)
                    if a and n >= 3 and n % 2: probs_T(n - 3, g0)
                if a: squares(g0); norm_T(g0)
                if a:
                    for n in range(FC // 2): gelu(n, g0)
                if b: y_square(g1); relu_square(g1); recept_tanh(g1)

            for dst, name in SMALL:
                act.dma_start(dst[:], io[name]).then_inc(small_w, 16)
            for dst, name in L1_LOADS:
                act.dma_start(dst[:], io[name]).then_inc(l1_w, 16)
            act.wait_ge(small_w, 16 * len(SMALL))
            act.wait_ge(setup, SETUP)
            both(0, None)
            both(1, 0)
            with act.Fori(2, GROUPS) as i:
                both(i, i - 1)
            both(None, GROUPS - 1)

        @blk.gpsimd
        def _(pool):
            tt = nc.gpsimd.tensor_tensor

            def residuals(g):
                pool.wait_ge(x_in, g * 16 + 16)
                if not first(g):
                    taken(pool, "out", g - 1)
                    taken(pool, "mlp", g - 1)
                for dst, row, done in ((x_ob, OB, xob_done), (x_b2, B2, xb2_done)):
                    tt(dst[:, :, :], x_tok[:, :, :], rows[:, row, :].unsqueeze(1).broadcast_to([P, TT, C]),
                       add).then_inc(done, 1)

            def normalise(n, g):
                pool.wait_ge(rden_done, g * NS + n + 1)
                p = prob[:, n % 4, :, :]
                tt(p, p, rden[:, n, :].unsqueeze(2).broadcast_to([P, 4, KEYS]), mult).then_inc(prob_done, 1)

            def rms_power(g):
                pool.wait_ge(ssm_done, g + 1)
                tt(rms[:, :], ssm[:, :], power[:, 0:TT], ALU.pow).then_inc(rms_done, 1)

            def ln_power(i, g):
                pool.wait_ge(vare_done, g * 2 + i + 1)
                tt(rstd[:, i, :], vare[:, i, :], power[:, 0:TT], ALU.pow).then_inc(rstd_done, 1)

            def first_states(g):
                if not first(g):
                    pool.wait_ge(state_done, g * S)
                nc.gpsimd.tensor_copy(kv[:, :, :, 0], s0[:, bass.ds(g, 1), :, :].rearrange(
                    "p g s a -> p (g s) a")).then_inc(s0_done, 1)

            def add_xa(f, g):
                taken(pool, f"mix{f}", g)
                m = mixed[:, f, :, :].rearrange("p h (b l) -> p (h b) l", l=L)
                tt(m, m, xa[:, :, :, 1:L + 1].rearrange("p h b l -> p (h b) l"), add).then_inc(mixed_done, 1)

            def read_state(t, g):
                if t == 0:
                    taken(pool, "r", g)
                pool.wait_ge(state_done, g * S + t + 1)
                tt(rs[:, t % NR, :], r1[:, :, :, :].rearrange("p h b l -> p (h b l)"), state[:, t % NR, :],
                   mult).then_inc(rs_done, 1)

            def gn_power(g):
                taken(pool, "var", g)
                tt(g_rstd[:, :], gv[:, :], power[:, :], ALU.pow).then_inc(grstd_done, 1)

            def both(g0, g1):
                a, b = g0 is not None, g1 is not None
                if b: ln_power(0, g1); first_states(g1)
                if a: residuals(g0)
                for n in range(NS + 1):
                    if b and n < MAA: add_xa(n, g1)
                    if a and n >= 1: normalise(n - 1, g0)
                if b: read_state(0, g1); read_state(1, g1); read_state(2, g1)
                if a: rms_power(g0)
                if b:
                    for t in range(3, S): read_state(t, g1)
                    gn_power(g1)
                    ln_power(1, g1)

            pool.wait_ge(small_w, 16 * len(SMALL))
            pool.wait_ge(setup, SETUP)
            both(0, None)
            pool.wait_ge(l1_w, 16 * len(L1_LOADS))
            both(1, 0)
            with pool.Fori(2, GROUPS) as i:
                both(i, i - 1)
            both(None, GROUPS - 1)

        @blk.vector
        def _(dve):
            tt, ts, stt = nc.vector.tensor_tensor, nc.vector.tensor_scalar, nc.vector.scalar_tensor_tensor

            def v_out(g):
                for n in range(2):
                    full(dve, f"v{n}", g)
                    for j in range(2):
                        last = tt(v_z[:, 2 * n + j, :, 0:4:3, :],
                                  psum(f"v{n}")[:, j * C:(j + 1) * C].rearrange("p (r a d) -> p r a d", a=2, d=DH),
                                  rows[:, VB, :].rearrange("p (r a d) -> p r a d", a=2, d=DH), add)
                    freed(last, f"v{n}")

            def mask_row(g):
                dve.wait_ge(mask_in, g * 16 + 16)
                full(dve, "v1", g)
                ts(mask[:, :, 0:L], mask_i[:, :, :], 0, MASKED, ALU.is_equal, mult).then_inc(mask_done, 1)

            def row_max(n, g):
                full(dve, f"s{n}", g)
                nc.vector.tensor_reduce(nmax[:, n, :], psum(f"s{n}")[:, :].rearrange("p (j k) -> p j k", j=4),
                                        AX.X, amax, negate=True).then_inc(nmax_done, 1)

            def reciprocals(n, g):
                taken(dve, f"s{n}", g)
                nc.vector.reciprocal(rden[:, n, :], den[:, n, :]).then_inc(rden_done, 1)

            def probs_T(n, g):
                full(dve, f"p{n}", g)
                freed(nc.vector.tensor_copy(prob_T[:, n // R, n % R, :, :],
                                            psum(f"p{n}")[:, :].rearrange("p (j q) -> p j q", j=4)), f"p{n}")

            def att_out(bp, g):
                full(dve, f"o{bp}", g)
                freed(nc.vector.tensor_copy(att_T[:, :, bp * P:(bp + 1) * P],
                                            psum(f"o{bp}")[:, 0:H * P].rearrange("p (h q) -> p h q", h=H)), f"o{bp}")

            def residual(use, dst, x, x_done, g):
                x_done(g)
                full(dve, use, g)
                freed(tt(dst[:, :, :], psum(use)[:, :].rearrange("p (t c) -> p t c", t=TT), x[:, :, :], add), use)

            def rms_mean(g):
                dve.wait_ge(ss_done, g + 1)
                ts(ssm[:, :], ss[:, :], 1.0 / C, EPS0, mult, add).then_inc(ssm_done, 1)

            def rms_norm(g):
                dve.wait_ge(rms_done, g + 1)
                taken(dve, "out", g)
                for t in range(TT):
                    last = ts(nrm[:, t, :], res[:, t, :], rms[:, t:t + 1], None, mult)
                last.then_inc(nrm_done, 1)

            def ln_stats(i, x, x_use, g):
                taken(dve, x_use, g)
                for t in range(TT):
                    last = nc.vector.bn_stats(stats[:, i, t, :], x[:, t, :])
                last.then_inc(stat_done, 1)
                dve.wait_ge(stat_done, g * 2 + i + 1)
                nc.vector.memset(carrier[:, :], 0.0)
                for t in range(TT):
                    last = nc.vector.bn_aggr(mv[:, i, t, :], stats[:, i, t, :])
                last.then_inc(mv_done, 1)
                dve.wait_ge(mv_done, g * 2 + i + 1)
                ts(vare[:, i, :], mv[:, i, :, 1], EPS1, None, add).then_inc(vare_done, 1)

            def ln_norm(i, x, g):
                dve.wait_ge(rstd_done, g * 2 + i + 1)
                for t in range(TT):
                    last = ts(xh[:, t, :], x[:, t, :], mv[:, i, t, 0:1], rstd[:, i, t:t + 1], sub, mult)
                last.then_inc(xh_done, 1)

            def shifted(i, use, x, d, w, bias, g):
                full(dve, use, g)
                nc.vector.tensor_copy(x[:, :, :, 0].rearrange("p h b -> p (h b)"),
                                      edge[:, bass.ds(g, 1), 1 - i, :].rearrange("p g a -> p (g a)")
                                      ).then_inc(edge_done, 1)
                for h in range(H):
                    last = ts(x[:, h, :, 1:L + 1], seqs(psum(use)[:, h * T:(h + 1) * T]), cols[:, w, h:h + 1],
                              cols[:, bias, h:h + 1], mult, add)
                freed(last, use)
                dve.wait_ge(edge_done, g * 2 + i + 1)
                taken(dve, use, g)
                tt(d[:, :, :, :].rearrange("p h b l -> p (h b) l"),
                   x[:, :, :, 0:L].rearrange("p h b l -> p (h b) l"),
                   x[:, :, :, 1:L + 1].rearrange("p h b l -> p (h b) l"), sub).then_inc(sx_done, 1)
                dve.wait_ge(sx_done, g * 2 + i + 1)

            def lerp(dst, x, d, col, h):
                return stt(seqs(dst[:, h, :]), d[:, h, :, :], cols[:, col, h:h + 1], x[:, h, :, 1:L + 1], mult, add)

            def maa_in(g):
                for h in range(H):
                    last = lerp(xx, xa, sx, MAAX, h)
                last.then_inc(xx_done, 1)

            def mix_m(f, g):
                full(dve, f"mix{f}", g)
                for h in range(H):
                    last = stt(mixed[:, f, h, :], psum(f"mix{f}")[:, h * T:(h + 1) * T], cols[:, MAA0 + f, h:h + 1],
                               sx[:, h, :, :].rearrange("p b l -> p (b l)"), add, mult)
                freed(last, f"mix{f}")

            def gate_out(g):
                dve.wait_ge(tg_done, g + 1)
                freed(stt(gate[:, :, :].rearrange("p h t -> p (h t)"), gate[:, :, :].rearrange("p h t -> p (h t)"),
                          1.0, psum("g")[:, :], add, mult), "g")

            def r_u_k(g):
                taken(dve, "k", g)
                taken(dve, "r", g)
                for h in range(H):
                    last = stt(ruk[:, h, :], k1[:, h, :, :].rearrange("p b l -> p (b l)"), cols[:, U, h:h + 1],
                               r1[:, h, :, :].rearrange("p b l -> p (b l)"), mult, mult)
                last.then_inc(ruk_done, 1)

            def bonus_out(g):
                taken(dve, "vc", g)
                full(dve, "bonus", g)
                freed(tt(bonus[:, :], psum("bonus")[:, :], v_c[:, :], mult), "bonus")

            def scan(t, g):
                full(dve, f"vr{t}", g)
                if t == 0:
                    dve.wait_ge(w_done, g + 1)
                    dve.wait_ge(s0_done, g + 1)
                freed(tt(kv[:, t, :, 1:L], k1[:, :, :, 0:L - 1].rearrange("p h b l -> p (h b) l"),
                         psum(f"vr{t}")[:, :].rearrange("p (a l) -> p a l", l=L)[:, :, 0:L - 1], mult), f"vr{t}")
                if not first(g) or t >= NR:
                    dve.wait_ge(rs_done, g * S + (t - NR + 1 if t >= NR else 0))
                taken(dve, f"vr{t}", g)
                nc.vector.tensor_tensor_scan(state[:, t % NR, :], w_sh[:, :, :, :].rearrange("p h b l -> p (h b l)"),
                                             kv[:, t, :, :].rearrange("p a l -> p (a l)"), 0.0, mult,
                                             add).then_inc(state_done, 1)

            def y_out(g):
                full(dve, "y", g)
                taken(dve, "bonus", g)
                freed(tt(yc[:, :, :].rearrange("p h t -> p (h t)"), psum("y")[:, :], bonus[:, :], add), "y")

            def var_out(g):
                full(dve, "var", g)
                freed(ts(gv[:, :], psum("var")[:, 0:TT * NH1], EPS1, None, add), "var")

            def widen(g):
                dve.wait_ge(grstd_done, g + 1)
                nc.vector.tensor_copy(g_wide[:, :, :].rearrange("p t (n s) -> p (t n) s", s=S),
                                      g_rstd[:, :].unsqueeze(2).broadcast_to([P, TT * NH1, S])
                                      ).then_inc(gwide_done, 1)

            def group_norm(g):
                full(dve, "rstd", g)
                freed(tt(z[:, :, :].rearrange("p h t -> p (h t)"), psum("rstd")[:, :],
                         yc[:, :, :].rearrange("p h t -> p (h t)"), mult), "rstd")
                taken(dve, "rstd", g)
                for h in range(H):
                    last = ts(z[:, h, :], z[:, h, :], gn_half[:, 0, h:h + 1], gn_half[:, 1, h:h + 1], mult, add)
                last.then_inc(z2_done, 1)
                dve.wait_ge(z2_done, g + 1)
                taken(dve, "g", g)
                tt(z[:, :, :], z[:, :, :], gate[:, :, :], mult).then_inc(z_done, 1)

            def ffn_in(g):
                for dst, col in ((xk2, FMK), (xr2, FMR)):
                    for h in range(H):
                        last = lerp(dst, xa, sx, col, h)
                last.then_inc(xkr_done, 1)

            def out(g):
                full(dve, "fv", g)
                taken(dve, "fr", g)
                freed(stt(tr[:, :, :].rearrange("p t c -> p (t c)"), tr[:, :, :].rearrange("p t c -> p (t c)"), 1.0,
                          psum("fv")[:, :], add, mult), "fv")
                if not first(g):
                    dve.wait_ge(out_done, g * 16)
                taken(dve, "fv", g)
                stt(o[:, :, :], tr[:, :, :], 0.5, x2[:, :, :], mult, add).then_inc(o_done, 1)

            def both(g0, g1):
                a, b = g0 is not None, g1 is not None
                if b:
                    ln_stats(0, x1, "mlp", g1)
                    ln_norm(0, x1, g1)
                    shifted(0, "xa", xa, sx, LN1W, LN1B, g1)
                    maa_in(g1)
                if a: v_out(g0); mask_row(g0)
                for n in range(NS + 3):
                    if a and n < NS: row_max(n, g0)
                    if b and n < MAA: mix_m(n, g1)
                    if a and 1 <= n <= NS: reciprocals(n - 1, g0)
                    if b and n == 8: gate_out(g1); r_u_k(g1)
                    if a and n >= 3 and n % 2 == 0: probs_T(n - 3, g0)
                    if a and n == 8: att_out(0, g0)
                if b: bonus_out(g1); scan(0, g1); scan(1, g1)
                if a: att_out(1, g0)
                if b: scan(2, g1)
                if a: residual("out", res, x_ob, lambda g: dve.wait_ge(xob_done, g + 1), g0)
                if b: scan(3, g1)
                if a: rms_mean(g0)
                if b: scan(4, g1)
                if a: rms_norm(g0)
                if b:
                    for t in range(5, S): scan(t, g1)
                    y_out(g1)
                    var_out(g1)
                    widen(g1)
                    group_norm(g1)
                    residual("wo", x2, x1, lambda g: None, g1)
                if a:
                    if b: taken(dve, "wo", g1)
                    residual("mlp", x1, x_b2, lambda g: dve.wait_ge(xb2_done, g + 1), g0)
                if b:
                    ln_stats(1, x2, "wo", g1)
                    ln_norm(1, x2, g1)
                    shifted(1, "xc", xa, sx, LN2W, LN2B, g1)
                    ffn_in(g1)
                    out(g1)

            nc.vector.memset(w_sh[:, :, :, 0], 0.0).then_inc(setup, 1)
            nc.vector.memset(v_z[:, :, :, :, :], 0.0).then_inc(setup, 1)
            nc.vector.memset(mask[:, :, L:KEYS], 0.0).then_inc(setup, 1)
            nc.vector.memset(ones[:, :], 1.0).then_inc(setup, 1)
            nc.vector.memset(power[:, :], -0.5).then_inc(setup, 1)
            dve.wait_ge(small_w, 16 * len(SMALL))
            ts(gn_half[:, :, :], cols[:, GNW:GNB + 1, :], 0.5, None, mult).then_inc(setup, 1)
            for par in range(2):
                last = ts(q_bias[:, :, par], cols[:, QB, :], parity[:, par:par + 1], None, mult)
            last.then_inc(setup, 1)
            dve.wait_ge(setup, SETUP)
            both(0, None)
            dve.wait_ge(l1_w, 16 * len(L1_LOADS))
            both(1, 0)
            with dve.Fori(2, GROUPS) as i:
                both(i, i - 1)
            both(None, GROUPS - 1)


def shape_constants():
    p = np.arange(P)
    same = (p[:, None] // S == p[None, :] // S).astype(np.float32)
    at = (p[None, :] % S == np.arange(S)[:, None]).astype(np.float32)
    return {
        "ident": np.eye(P, dtype=np.float32),
        "block": same,
        "centre": np.eye(P, dtype=np.float32) - same / S,
        "mean16": np.ascontiguousarray((p[:, None] // S == np.arange(P // S)[None, :]).astype(np.float32) / S),
        "rep": np.ascontiguousarray((same[:, None, :] * at.T[:, :, None]).astype(np.float32)),
        "fold": np.ascontiguousarray((same[:, None, :] * (at[None, :, :] - 1 / S)).astype(np.float32)),
        "parity": np.stack([(p // DH % 2 == i).astype(np.float32) / DH for i in range(2)], axis=1),
    }


def kernel(**inputs):
    import concourse.bacc as bacc
    from concourse.bass_utils import run_bass_kernel_spmd

    a = {k: np.asarray(v) for k, v in inputs.items()}
    l0 = {k[len("L0_xattn_"):]: v for k, v in a.items() if k.startswith("L0_xattn_")}
    l1 = {k[len("L1_xattn_"):]: v for k, v in a.items() if k.startswith("L1_xattn_")}

    def rows_of(w):
        return np.ascontiguousarray(w.reshape(-1, P, w.shape[1]).transpose(1, 0, 2))

    def half_cols(v):
        return np.ascontiguousarray(v.reshape(-1, H, P).transpose(2, 0, 1))

    x, ctx = a["x"], a["ctx_2048"]
    h = np.concatenate([ctx, x], axis=1)
    h_T = h.reshape(GROUPS, GB, KEYS, H, P).transpose(0, 4, 3, 1, 2)
    vectors = [l0["q_b"], l0["kv_b"][0::2], l0["postnorm_w"], l1["ln1_w"], l1["ln1_b"], l1["ln2_w"], l1["ln2_b"],
               l1["maa_x"], l1["maa_w"], l1["maa_k"], l1["maa_v"], l1["maa_r"], l1["maa_g"], l1["time_decay"],
               l1["faaaa"].reshape(C), l1["gn_w"], l1["gn_b"], l1["fmaa_k"], l1["fmaa_r"]]
    s0 = ctx[:, 2:2 + S, :].reshape(GROUPS, GB, H, P, S).transpose(3, 0, 4, 2, 1)
    edge = ctx[:, 0:2, :].reshape(GROUPS, GB, 2, H, P).transpose(4, 0, 2, 3, 1)
    arrays = {
        "x": np.ascontiguousarray(x.reshape(B * L, C)),
        "h_T": np.ascontiguousarray(h_T).reshape(GROUPS, P, H * GB * KEYS),
        "q_w": rows_of(l0["q_w"]), "k_w": rows_of(l0["kv_w"][:, 0::2]), "v_w": rows_of(l0["kv_w"][:, 1::2]),
        "out_w": rows_of(l0["out_w"]), "w1": rows_of(l0["mlp_w1"]), "w2": rows_of(l0["mlp_w2"]),
        "b1": np.ascontiguousarray(l0["mlp_b1"].reshape(FC, P).T),
        "rows": np.ascontiguousarray(np.broadcast_to(
            np.stack([l0["kv_b"][1::2], l0["out_b"], l0["mlp_b2"]])[None], (P, 3, C))),
        "cols": half_cols(np.stack(vectors)),
        "mask": np.ascontiguousarray(a["mask_BxS2_ik0"]).reshape(1, B, L),
        "maa_w1": rows_of(l1["maa_w1"]),
        "maa_w2": np.ascontiguousarray(l1["maa_w2"][0:4].reshape(P, C)),
        "maa_w2g": np.ascontiguousarray(l1["maa_w2"][4]),
        "decay_w1": rows_of(l1["decay_w1"]), "decay_w2": l1["decay_w2"],
        "wr": rows_of(l1["Wr"].T), "wk": rows_of(l1["Wk"].T), "wv": rows_of(l1["Wv"].T), "wg": rows_of(l1["Wg"].T),
        "wo": rows_of(l1["Wo"].T), "fwk": rows_of(l1["fWk"].T), "fwr": rows_of(l1["fWr"].T),
        "fwv": rows_of(l1["fWv"].T),
        "s0": np.ascontiguousarray(s0).reshape(P, GROUPS, S, H * GB),
        "edge": np.ascontiguousarray(edge).reshape(P, GROUPS, 2, H * GB),
        **shape_constants(),
    }
    nc = bacc.Bacc("TRN2", target_bir_lowering=False, num_devices=1)
    io = {n: nc.dram_tensor(f"in_{n}", v.shape, mybir.dt.from_np(v.dtype), kind="ExternalInput").ap()
          for n, v in arrays.items()}
    io["out"] = nc.dram_tensor("out", (B * L, C), mybir.dt.float32, kind="ExternalOutput").ap()
    build(nc, io)
    r = run_bass_kernel_spmd(nc, [{f"in_{n}": v for n, v in arrays.items()}], core_ids=[0])
    return r.results[0]["out"].reshape(B, L, C)
```

```python
from contextlib import ExitStack

import numpy as np

import concourse.bass as bass
from concourse import mybir

B, L, C = 32, 64, 256
KEYS = 2 * L
NH0, DH = 16, 16
NH1, S = 32, 8
F = 4 * C
MAA = 5
DM, DD = 32, 64
P = 128
H = C // P
GB = 4
T = GB * L
TT = T // P
GROUPS = B // GB
R = 4
NS = (GB // 2) * R
FC = F // P
EPS0, EPS1 = 1e-6, 1e-5
MASKED = -1e30

BANK_USES = [
    ["q", "v1", "s1", "s3", "s5", "s7", "out", "m2"],
    ["k0", "s0", "s2", "s4", "s6", "norm", "m3"],
    ["k1", "p0", "p2", "p4", "p5", "p7", "m0", "mlp"],
    ["v0", "p1", "p3", "o0", "p6", "o1", "m1"],
    ["xa", "mix1", "mix4", "decay2", "g", "vr0", "vr3", "vr6", "rstd"],
    ["maa", "mix2", "decay1", "v", "vc", "vr1", "vr4", "vr7", "wo"],
    ["mix0", "mix3", "k", "r", "bonus", "vr2", "vr5", "var"],
    ["y", "xc", "fk", "fr", "fv"],
]
BANK_OF = {use: (b, k, len(uses)) for b, uses in enumerate(BANK_USES) for k, use in enumerate(uses)}
SETUP = 7


def build(nc, io):
    f32, f32r = mybir.dt.float32, mybir.dt.float32r
    bf16, i32 = mybir.dt.bfloat16, mybir.dt.int32
    ALU, ACT, AX = mybir.AluOpType, mybir.ActivationFunctionType, mybir.AxisListType
    mult, add, sub, amax = ALU.mult, ALU.add, ALU.subtract, ALU.max

    with ExitStack() as ctx:
        def sb(name, shape, dt=f32):
            return ctx.enter_context(nc.sbuf_tensor(name, shape, dt))

        def sem(name):
            return ctx.enter_context(nc.semaphore(name))

        q_w, k_w, v_w, out_w = (sb(n, [P, H, C]) for n in ("q_w", "k_w", "v_w", "out_w"))
        w1 = sb("w1", [P, H, F])
        w2 = sb("w2", [P, FC, C])
        maa_w1 = sb("maa_w1", [P, H, MAA * DM])
        maa_w2 = sb("maa_w2", [P, C])
        maa_w2g = sb("maa_w2g", [DM, C])
        decay_w1 = sb("decay_w1", [P, H, DD])
        decay_w2 = sb("decay_w2", [DD, C])
        wr, wk, wv, wg, wo, fwk, fwr, fwv = (
            sb(n, [P, H, C]) for n in ("wr", "wk", "wv", "wg", "wo", "fwk", "fwr", "fwv"))
        cols = sb("cols", [P, 19, H])
        (QB, KB, POST, LN1W, LN1B, LN2W, LN2B, MAAX, MAA0, TD, U, GNW, GNB, FMK, FMR) = (
            0, 1, 2, 3, 4, 5, 6, 7, 8, 13, 14, 15, 16, 17, 18)
        b1 = sb("b1", [P, FC])
        rows = sb("rows", [P, 3, C])
        VB, OB, B2 = 0, 1, 2
        ident = sb("ident", [P, P])
        block = sb("block", [P, P])
        centre = sb("centre", [P, P], f32r)
        mean16 = sb("mean16", [P, P // S])
        rep = sb("rep", [P, S, P], f32r)
        fold = sb("fold", [P, S, P])
        parity = sb("parity", [P, 2])
        q_bias = sb("q_bias", [P, H, 2])
        gn_half = sb("gn_half", [P, 2, H])
        power = sb("power", [P, TT])
        ones = sb("ones", [P, P], bf16)
        mask_i = sb("mask_i", [P, GB, L], i32)
        mask = sb("mask", [P, GB, KEYS], bf16)
        s0 = sb("s0", [P, GROUPS, S, H * GB])
        edge = sb("edge", [P, GROUPS, 2, H * GB])

        kv = sb("kv", [P, S, H * GB, L])
        h_T = sb("h_T", [P, H, GB, KEYS])
        x_tok = sb("x_tok", [P, TT, C])
        x_ob, x_b2 = x_tok, sb("x_b2", [P, TT, C])
        q_T = sb("q_T", [P, H, GB, 2, L])
        k_T = sb("k_T", [P, H, GB, KEYS])
        v_z = sb("v_z", [P, GB, H * R, 4, DH])
        nmax = sb("nmax", [P, NS, 4])
        den = sb("den", [P, NS, 4])
        rden = sb("rden", [P, NS, 4])
        prob = sb("prob", [P, 4, 4, KEYS])
        prob_T = sb("prob_T", [P, GB // 2, R, 4, P])
        att_T = sb("att_T", [P, H, T])
        nrm, res = (prob[:, i, :, :].rearrange("p j (a c) -> p (j a) c", a=1).rearrange(
            "p (t m) c -> p t (m c)", t=TT) for i in (0, 1))
        n_T = prob[:, 2, :, :].rearrange("p (h m) c -> p h (m c)", h=H)
        ss, ssm, rms = sb("ss", [P, TT]), sb("ssm", [P, TT]), sb("rms", [P, TT])
        hid = sb("hid", [P, FC, T])
        x1 = sb("x1", [P, TT, C])
        x2 = sb("x2", [P, TT, C])
        stats = sb("stats", [P, 2, TT, 6])
        carrier = sb("carrier", [1, 1])
        mv = sb("mv", [P, 2, TT, 2])
        vare, rstd = sb("vare", [P, 2, TT]), sb("rstd_ln", [P, 2, TT])
        xh, xh2 = sb("xh", [P, TT, C]), sb("xh2", [P, TT, C])
        xa = sb("xa", [P, H, GB, L + 1])
        g_wide = xh
        sx = sb("sx", [P, H, GB, L])
        xx = sb("xx", [P, H, T])
        th, thg = sb("th", [P, T]), sb("thg", [DM, T])
        mixed = sb("mixed", [P, MAA, H, T])
        d1 = sb("d1", [DD, T])
        w_sh = sb("w_sh", [P, H, GB, L])
        k1, r1 = sb("k1", [P, H, GB, L]), sb("r1", [P, H, GB, L])
        v_hi, v_lo = sb("v_hi", [P, H * T], f32r), sb("v_lo", [P, H * T], f32r)
        gate = sb("gate", [P, H, T])
        ew = gate[:, :, :].rearrange("p h (b l) -> p h b l", l=L)
        v_c = sb("v_c", [P, H * T])
        ruk, bonus = sb("ruk", [P, H, T]), sb("bonus", [P, H * T])
        NR = 3
        state = sb("state", [P, NR, H * T])
        rs = sb("rs", [P, NR, H * T])
        yc = sb("yc", [P, H, T])
        sq = ruk
        gv, g_rstd, g_t = (sb(n, [P, TT * NH1]) for n in ("gv", "g_rstd", "g_t"))
        z = sb("z", [P, H, T])
        xk2, xr2 = sb("xk2", [P, H, T]), sb("xr2", [P, H, T])
        kk = z
        tr, o = xh2, sb("o", [P, TT, C])

        bank = [ctx.enter_context(nc.psum_tensor(f"bank{b}", [P, 512], f32)) for b in range(8)]
        bank_full = [sem(f"bank_full{b}") for b in range(8)]
        bank_free = [sem(f"bank_free{b}") for b in range(8)]

        def psum(use):
            return bank[BANK_OF[use][0]]

        def first(g):
            return isinstance(g, int) and g == 0

        def full(eng, use, g):
            b, k, n = BANK_OF[use]
            eng.wait_ge(bank_full[b], g * n + (k + 1))

        def room(eng, use, g):
            b, k, n = BANK_OF[use]
            if not first(g) or k:
                eng.wait_ge(bank_free[b], g * n + k)

        def taken(eng, use, g):
            b, k, n = BANK_OF[use]
            eng.wait_ge(bank_free[b], g * n + (k + 1))

        def filled(ins, use):
            ins.then_inc(bank_full[BANK_OF[use][0]], 1)

        def freed(ins, use):
            ins.then_inc(bank_free[BANK_OF[use][0]], 1)

        l0_w, l1_w, small_w = sem("l0_w"), sem("l1_w"), sem("small_w")
        mask_in, mask_done = sem("mask_in"), sem("mask_done")
        h_in, x_in, out_done = sem("h_in"), sem("x_in"), sem("out_done")
        setup = sem("setup")
        nmax_done = sem("nmax_done")
        rden_done = sem("rden_done")
        prob_done = sem("prob_done")
        xob_done, xb2_done = sem("xob_done"), sem("xb2_done")
        ss_done, ssm_done, rms_done, nrm_done = sem("ss_done"), sem("ssm_done"), sem("rms_done"), sem("nrm_done")
        stat_done, mv_done = sem("stat_done"), sem("mv_done")
        vare_done, rstd_done, xh_done = sem("vare_done"), sem("rstd_done"), sem("xh_done")
        edge_done, sx_done, xx_done = sem("edge_done"), sem("sx_done"), sem("xx_done")
        mixed_done = sem("mixed_done")
        w_done, tg_done, ruk_done = sem("w_done"), sem("tg_done"), sem("ruk_done")
        s0_done, state_done, rs_done = sem("s0_done"), sem("state_done"), sem("rs_done")
        sq_done, newton_done, gwide_done, z2_done, z_done = sem("sq_done"), sem("newton_done"), sem("gwide_done"), sem("z2_done"), sem("z_done")
        vhi_done, l1_const = sem("vhi_done"), sem("l1_const")
        xkr_done, kk_done, o_done = sem("xkr_done"), sem("kk_done"), sem("o_done")

        def seqs(ap):
            return ap.rearrange("p (a l) -> p a l", l=L)

        blk = ctx.enter_context(nc.Block())

        L0_LOADS = [(q_w, "q_w"), (k_w, "k_w"), (v_w, "v_w")]
        L0_LATER = [(ident, "ident"), (out_w, "out_w"), (w1, "w1"), (w2, "w2")]
        SMALL = [(b1, "b1"), (rows, "rows"), (cols, "cols"), (parity, "parity")]
        L1_LOADS = [(maa_w1, "maa_w1"), (maa_w2, "maa_w2"), (maa_w2g, "maa_w2g"), (decay_w1, "decay_w1"),
                    (decay_w2, "decay_w2"), (wr, "wr"), (wk, "wk"), (wv, "wv"), (wg, "wg"), (wo, "wo"),
                    (fwk, "fwk"), (fwr, "fwr"), (fwv, "fwv"), (block, "block"), (mean16, "mean16"), (fold, "fold"),
                    (kv[:, 0:2, :, :].rearrange("p s a l -> p (s a l)"), "rep"),
                    (kv[:, 2, 0:2, :].rearrange("p a l -> p (a l)"), "centre"), (s0, "s0"), (edge, "edge")]

        @blk.sync
        def _(sp):
            def load_h(g):
                if not first(g):
                    full(sp, "v1", g - 1)
                sp.dma_start(h_T[:, :, :, :], io["h_T"][bass.ds(g, 1), :, :].rearrange(
                    "g p (h b k) -> p (g h) b k", h=H, b=GB)).then_inc(h_in, 16)

            def load_mask(g):
                if not first(g):
                    sp.wait_ge(mask_done, g)
                sp.dma_start(mask_i[:, :, :], io["mask"][:, bass.ds(g * GB, GB), :].broadcast_to([P, GB, L])).then_inc(mask_in, 16)

            def load_x(g):
                if not first(g):
                    taken(sp, "out", g - 1)
                sp.dma_start(x_tok[:, :, :], io["x"][bass.ds(g * T, T), :].rearrange(
                    "(t p) c -> p t c", p=P)).then_inc(x_in, 16)

            def store(g):
                sp.wait_ge(o_done, g + 1)
                sp.dma_start(io["out"][bass.ds(g * T, T), :].rearrange("(t p) c -> p t c", p=P),
                             o[:, :, :]).then_inc(out_done, 16)

            for dst, name in L0_LOADS:
                sp.dma_start(dst[:, :, :], io[name]).then_inc(l0_w, 16)
            load_h(0)
            load_mask(0)
            load_x(0)
            for dst, name in L0_LATER:
                sp.dma_start(dst[:], io[name]).then_inc(l0_w, 16)
            load_h(1)
            load_mask(1)
            load_x(1)
            with sp.Fori(2, GROUPS) as i:
                load_h(i)
                load_mask(i)
                load_x(i)
                store(i - 2)
            for g in range(GROUPS - 2, GROUPS):
                store(g)
            sp.wait_ge(out_done, 16 * GROUPS)

        @blk.tensor
        def _(pe):
            mm = nc.tensor.matmul

            def project_T(use, w, x, g):
                room(pe, use, g)
                for m in range(H):
                    for k in range(H):
                        last = mm(psum(use)[:, m * T:(m + 1) * T], w[:, k, m * P:(m + 1) * P], x[:, k, :],
                                  start=k == 0, stop=k == H - 1)
                filled(last, use)

            def project_tok(use, x, w, g, chunks=H, tiles=range(TT)):
                if tiles[0] == 0:
                    room(pe, use, g)
                for t in tiles:
                    for k in range(chunks):
                        last = mm(psum(use)[:, t * C:(t + 1) * C], x[:, k, t * P:(t + 1) * P], w[:, k, :],
                                  start=k == 0, stop=k == chunks - 1)
                if tiles[-1] == TT - 1:
                    filled(last, use)

            def turn(use, x, g):
                room(pe, use, g)
                for t in range(TT):
                    for h in range(H):
                        last = nc.tensor.transpose(psum(use)[:, h * T + t * P:h * T + (t + 1) * P],
                                                   x[:, t, h * P:(h + 1) * P], ident[:, :])
                filled(last, use)

            def q_proj(g):
                pe.wait_ge(h_in, g * 16 + 16)
                room(pe, "q", g)
                for m in range(H):
                    for k in range(H):
                        last = mm(psum("q")[:, m * T:(m + 1) * T], q_w[:, k, m * P:(m + 1) * P],
                                  h_T[:, k, :, L:KEYS], start=k == 0, stop=k == H - 1)
                filled(last, "q")

            def k_proj(g):
                for m in range(H):
                    room(pe, f"k{m}", g)
                    for k in range(H):
                        last = mm(psum(f"k{m}")[:, :], k_w[:, k, m * P:(m + 1) * P], h_T[:, k, :, :],
                                  start=k == 0, stop=k == H - 1)
                    filled(last, f"k{m}")

            def v_proj(g):
                for n in range(2):
                    room(pe, f"v{n}", g)
                    for j in range(2):
                        for k in range(H):
                            last = mm(psum(f"v{n}")[:, j * C:(j + 1) * C], h_T[:, k, 2 * n + j, :], v_w[:, k, :],
                                      start=k == 0, stop=k == H - 1)
                    filled(last, f"v{n}")

            def scores(n, g):
                bp, r = n // R, n % R
                if n == 0:
                    taken(pe, "q", g)
                    taken(pe, "k0", g)
                    taken(pe, "k1", g)
                    pe.wait_ge(mask_done, g + 1)
                room(pe, f"s{n}", g)
                out = psum(f"s{n}")
                for j in range(4):
                    b, h = 2 * bp + j // 2, j % 2
                    mm(out[:, j * P:(j + 1) * P], ones[32 * r:32 * r + 1, :], mask[32 * r:32 * r + 1, b, :],
                       start=True, stop=False)
                    last = mm(out[:, j * P:(j + 1) * P], q_T[32 * r:32 * r + 32, h, b, :, :],
                              k_T[32 * r:32 * r + 32, h, b, :], start=False, stop=True)
                filled(last, f"s{n}")

            def turn_probs(n, g):
                pe.wait_ge(prob_done, g * NS + n + 1)
                room(pe, f"p{n}", g)
                for j in range(4):
                    last = nc.tensor.transpose(psum(f"p{n}")[:, j * P:(j + 1) * P], prob[:, n % 4, j, :], ident[:, :])
                filled(last, f"p{n}")

            def attend(bp, g):
                taken(pe, f"p{R * bp + 2}", g)
                taken(pe, f"p{R * bp + 3}", g)
                if bp:
                    taken(pe, "v1", g)
                room(pe, f"o{bp}", g)
                for j in range(4):
                    b, h = 2 * bp + j // 2, j % 2
                    c = h * P + (j // 2) * L
                    for par in range(2):
                        for r in range(R):
                            last = mm(psum(f"o{bp}")[32 * r:32 * r + 32, c:c + L],
                                      v_z[:, b, h * R + r, 2 * par:2 * par + 2, :],
                                      prob_T[:, bp, r, j, par * L:(par + 1) * L], start=par == 0, stop=par == 1)
                filled(last, f"o{bp}")

            def out_proj(g):
                taken(pe, "o1", g)
                project_tok("out", att_T, out_w, g)

            def turn_norm(g):
                pe.wait_ge(nrm_done, g + 1)
                turn("norm", nrm, g)

            def mlp_up(n, g):
                if n == 0:
                    taken(pe, "norm", g)
                room(pe, f"m{n}", g)
                for j in range(2):
                    c = (2 * n + j) * P
                    for k in range(H):
                        last = mm(psum(f"m{n}")[:, j * T:(j + 1) * T], w1[:, k, c:c + P], n_T[:, k, :],
                                  start=k == 0, stop=k == H - 1)
                filled(last, f"m{n}")

            def mlp_down(t, g):
                if t == 0:
                    for n in range(FC // 2):
                        taken(pe, f"m{n}", g)
                project_tok("mlp", hid, w2, g, FC, [t])

            def turn_xa(g):
                pe.wait_ge(xh_done, g * 2 + 1)
                turn("xa", xh, g)

            def maa(g):
                pe.wait_ge(xx_done, g + 1)
                room(pe, "maa", g)
                for k in range(H):
                    mm(psum("maa")[:, 0:T], maa_w1[:, k, 0:P], xx[:, k, :], start=k == 0, stop=k == H - 1)
                for k in range(H):
                    last = mm(psum("maa")[0:DM, T:2 * T], maa_w1[:, k, P:P + DM], xx[:, k, :],
                              start=k == 0, stop=k == H - 1)
                filled(last, "maa")

            def mix(f, g):
                if f == 0:
                    taken(pe, "maa", g)
                room(pe, f"mix{f}", g)
                for h in range(H):
                    if f < 4:
                        w, x = maa_w2[32 * f:32 * f + 32, h * P:(h + 1) * P], th[32 * f:32 * f + 32, :]
                    else:
                        w, x = maa_w2g[:, h * P:(h + 1) * P], thg[:, :]
                    last = mm(psum(f"mix{f}")[:, h * T:(h + 1) * T], w, x, start=True, stop=True)
                filled(last, f"mix{f}")

            def decay1(g):
                pe.wait_ge(mixed_done, g * MAA + 1)
                room(pe, "decay1", g)
                for k in range(H):
                    last = mm(psum("decay1")[0:DD, 0:T], decay_w1[:, k, :], mixed[:, 0, k, :],
                              start=k == 0, stop=k == H - 1)
                filled(last, "decay1")

            def decay2(g):
                taken(pe, "decay1", g)
                room(pe, "decay2", g)
                for h in range(H):
                    last = mm(psum("decay2")[:, h * T:(h + 1) * T], decay_w2[:, h * P:(h + 1) * P], d1[:, :],
                              start=True, stop=True)
                filled(last, "decay2")

            def proj(use, f, w, g):
                pe.wait_ge(mixed_done, g * MAA + f + 1)
                project_T(use, w, mixed[:, f, :, :], g)

            def v_centred(g):
                taken(pe, "v", g)
                room(pe, "vc", g)
                mm(psum("vc")[:, :], centre[:, :], v_hi[:, :], start=True, stop=False)
                filled(mm(psum("vc")[:, :], centre[:, :], v_lo[:, :], start=False, stop=True), "vc")

            def bonus_sum(g):
                pe.wait_ge(ruk_done, g + 1)
                room(pe, "bonus", g)
                filled(mm(psum("bonus")[:, :], block[:, :], ruk[:, :, :], start=True, stop=True), "bonus")

            def v_rep(t, g):
                room(pe, f"vr{t}", g)
                mm(psum(f"vr{t}")[:, :], rep[:, t, :], v_hi[:, :], start=True, stop=False)
                filled(mm(psum(f"vr{t}")[:, :], rep[:, t, :], v_lo[:, :], start=False, stop=True), f"vr{t}")

            def y_sum(t, g):
                pe.wait_ge(rs_done, g * S + t + 1)
                if t == 0:
                    room(pe, "y", g)
                last = mm(psum("y")[:, :], fold[:, t, :], rs[:, t % NR, :], start=t == 0, stop=t == S - 1)
                if t == S - 1:
                    filled(last, "y")

            def variance(g):
                pe.wait_ge(sq_done, g + 1)
                room(pe, "var", g)
                n = P // S
                for t in range(TT):
                    for h in range(H):
                        c = (t * H + h) * n
                        last = mm(psum("var")[:, c:c + n], sq[:, h, t * P:(t + 1) * P], mean16[:, :],
                                  start=True, stop=True)
                filled(last, "var")

            def turn_rstd(g):
                pe.wait_ge(gwide_done, g + 1)
                room(pe, "rstd", g)
                for t in range(TT):
                    for h in range(H):
                        last = nc.tensor.transpose(psum("rstd")[:, h * T + t * P:h * T + (t + 1) * P],
                                                   g_wide[:, t, h * P:(h + 1) * P], ident[:, :])
                filled(last, "rstd")

            def w_out(g):
                pe.wait_ge(z_done, g + 1)
                project_tok("wo", z, wo, g)

            def turn_xc(g):
                pe.wait_ge(xh_done, g * 2 + 2)
                turn("xc", xh2, g)

            def ffn_key(g):
                pe.wait_ge(xkr_done, g + 1)
                project_T("fk", fwk, xk2, g)

            def ffn_value(g):
                pe.wait_ge(kk_done, g + 1)
                project_tok("fv", kk, fwv, g)

            def both(g0, g1, g2):
                a, b, c = (g is not None for g in (g0, g1, g2))
                if a: q_proj(g0); k_proj(g0)
                if c: turn_xc(g2)
                if a: v_proj(g0)
                if b: turn_xa(g1)
                if c: ffn_key(g2); project_tok("fr", xr2, fwr, g2)
                if b: maa(g1)
                if c: ffn_value(g2)
                for n in range(NS + 3):
                    if a and n < NS: scores(n, g0)
                    if b and n < MAA: mix(n, g1)
                    if b and n == 4: decay1(g1)
                    if b and n == 5: proj("v", 2, wv, g1)
                    if b and n == 6: proj("k", 1, wk, g1); decay2(g1)
                    if b and n == 7: proj("r", 3, wr, g1)
                    if b and n == 8: proj("g", 4, wg, g1); v_centred(g1)
                    if a and n >= 3: turn_probs(n - 3, g0)
                    if a and n == R + 3: attend(0, g0)
                if b: bonus_sum(g1); v_rep(0, g1); v_rep(1, g1)
                if a: attend(1, g0)
                if b: v_rep(2, g1)
                if a: out_proj(g0)
                for t in range(S):
                    if b:
                        y_sum(t, g1)
                        if t + 3 < S: v_rep(t + 3, g1)
                    if a and t == 2: turn_norm(g0)
                    if a and t >= 4: mlp_up(t - 4, g0)
                if b: variance(g1)
                if a: mlp_down(0, g0)
                if b: turn_rstd(g1)
                if a: mlp_down(1, g0)
                if b: w_out(g1)

            pe.wait_ge(l0_w, 16 * (len(L0_LOADS) + len(L0_LATER)))
            pe.wait_ge(setup, SETUP)
            both(0, None, None)
            pe.wait_ge(l1_w, 16 * len(L1_LOADS))
            pe.wait_ge(l1_const, 2)
            both(1, 0, None)
            with pe.Fori(2, GROUPS) as i:
                both(i, i - 1, i - 2)
            both(None, GROUPS - 1, GROUPS - 2)
            both(None, None, GROUPS - 1)

        @blk.scalar
        def _(act):
            fn = nc.scalar.activation

            def q_out(g):
                full(act, "q", g)
                for h in range(H):
                    for par in range(2):
                        last = fn(q_T[:, h, :, par, :], seqs(psum("q")[:, h * T:(h + 1) * T]), ACT.Identity,
                                  bias=q_bias[:, h, par:par + 1], scale=parity[:, par:par + 1])
                freed(last, "q")

            def k_out(g):
                for m in range(H):
                    full(act, f"k{m}", g)
                    freed(fn(k_T[:, m, :, :], psum(f"k{m}")[:, :].rearrange("p (b k) -> p b k", b=GB),
                             ACT.Identity, bias=cols[:, KB, m:m + 1]), f"k{m}")

            def exps(n, g):
                act.wait_ge(nmax_done, g * NS + n + 1)
                for j in range(4):
                    last = fn(prob[:, n % 4, j, :], psum(f"s{n}")[:, j * P:(j + 1) * P], ACT.Exp,
                              bias=nmax[:, n, j:j + 1], accum_out=den[:, n, j:j + 1])
                freed(last, f"s{n}")

            def probs_T(n, g):
                full(act, f"p{n}", g)
                freed(fn(prob_T[:, n // R, n % R, :, :], psum(f"p{n}")[:, :].rearrange("p (j q) -> p j q", j=4),
                         ACT.Copy), f"p{n}")

            def squares(g):
                taken(act, "out", g)
                for t in range(TT):
                    last = fn(nrm[:, t, :], res[:, t, :], ACT.Square, accum_out=ss[:, t:t + 1])
                last.then_inc(ss_done, 1)

            def norm_T(g):
                full(act, "norm", g)
                for h in range(H):
                    last = fn(n_T[:, h, :], psum("norm")[:, h * T:(h + 1) * T], ACT.Identity,
                              scale=cols[:, POST, h:h + 1])
                freed(last, "norm")

            def gelu(n, g):
                full(act, f"m{n}", g)
                for j in range(2):
                    c = 2 * n + j
                    last = fn(hid[:, c, :], psum(f"m{n}")[:, j * T:(j + 1) * T], ACT.Gelu_apprx_tanh,
                              bias=b1[:, c:c + 1])
                freed(last, f"m{n}")

            def maa_tanh(g):
                full(act, "maa", g)
                fn(th[:, :], psum("maa")[:, 0:T], ACT.Tanh)
                freed(fn(thg[:, :], psum("maa")[0:DM, T:2 * T], ACT.Tanh), "maa")

            def decay_tanh(g):
                full(act, "decay1", g)
                freed(fn(d1[:, :], psum("decay1")[0:DD, 0:T], ACT.Tanh), "decay1")

            def decays(g):
                full(act, "decay2", g)
                for h in range(H):
                    last = fn(ew[:, h, :, :], seqs(psum("decay2")[:, h * T:(h + 1) * T]), ACT.Exp,
                              bias=cols[:, TD, h:h + 1])
                freed(last, "decay2")
                taken(act, "decay2", g)
                fn(w_sh[:, :, :, 1:L].rearrange("p h b l -> p (h b) l"),
                   ew[:, :, :, 0:L - 1].rearrange("p h b l -> p (h b) l"), ACT.Exp, scale=-1.0).then_inc(w_done, 1)

            def keep(use, dst, g):
                full(act, use, g)
                freed(fn(dst, psum(use)[:, :], ACT.Copy), use)

            def v_high(g):
                full(act, "v", g)
                fn(v_hi[:, :], psum("v")[:, :], ACT.Copy).then_inc(vhi_done, 1)

            def gate_tanh(g):
                full(act, "g", g)
                act.wait_ge(w_done, g + 1)
                fn(gate[:, :, :], psum("g")[:, :], ACT.Tanh, scale=0.5).then_inc(tg_done, 1)

            def y_square(g):
                taken(act, "y", g)
                fn(sq[:, :, :], yc[:, :, :], ACT.Square).then_inc(sq_done, 1)

            def relu_square(g):
                full(act, "fk", g)
                freed(fn(kk[:, :, :], psum("fk")[:, :], ACT.Relu), "fk")
                taken(act, "fk", g)
                fn(kk[:, :, :], kk[:, :, :], ACT.Square).then_inc(kk_done, 1)

            def recept_tanh(g):
                full(act, "fr", g)
                freed(fn(tr[:, :, :], psum("fr")[:, :], ACT.Tanh, scale=0.5), "fr")

            def both(g0, g1, g2):
                a, b, c = (g is not None for g in (g0, g1, g2))
                if a: q_out(g0); k_out(g0)
                if c: relu_square(g2); recept_tanh(g2)
                if b: maa_tanh(g1)
                for n in range(NS + 3):
                    if a and n < NS: exps(n, g0)
                    if b and n == 4: decay_tanh(g1)
                    if b and n == 5: v_high(g1)
                    if b and n == 6: keep("k", k1[:, :, :, :], g1); decays(g1)
                    if b and n == 7: keep("r", r1[:, :, :, :], g1)
                    if b and n == 8: gate_tanh(g1); keep("vc", v_c[:, :], g1)
                    if a and n >= 3 and n % 2: probs_T(n - 3, g0)
                if a: squares(g0); norm_T(g0)
                if a:
                    for n in range(FC // 2): gelu(n, g0)
                if b: y_square(g1)

            for dst, name in SMALL:
                act.dma_start(dst[:], io[name]).then_inc(small_w, 16)
            for dst, name in L1_LOADS:
                act.dma_start(dst[:], io[name]).then_inc(l1_w, 16)
            act.wait_ge(small_w, 16 * len(SMALL))
            act.wait_ge(setup, SETUP)
            both(0, None, None)
            both(1, 0, None)
            with act.Fori(2, GROUPS) as i:
                both(i, i - 1, i - 2)
            both(None, GROUPS - 1, GROUPS - 2)
            both(None, None, GROUPS - 1)

        @blk.gpsimd
        def _(pool):
            tt = nc.gpsimd.tensor_tensor

            def residuals(g):
                pool.wait_ge(x_in, g * 16 + 16)
                if not first(g):
                    taken(pool, "mlp", g - 1)
                for dst, row, done in ((x_b2, B2, xb2_done), (x_ob, OB, xob_done)):
                    tt(dst[:, :, :], x_tok[:, :, :], rows[:, row, :].unsqueeze(1).broadcast_to([P, TT, C]),
                       add).then_inc(done, 1)
                    if row == B2:
                        pool.wait_ge(xb2_done, g + 1)

            def normalise(n, g):
                pool.wait_ge(rden_done, g * NS + n + 1)
                p = prob[:, n % 4, :, :]
                tt(p, p, rden[:, n, :].unsqueeze(2).broadcast_to([P, 4, KEYS]), mult).then_inc(prob_done, 1)

            def rms_power(g):
                pool.wait_ge(ssm_done, g + 1)
                tt(rms[:, :], ssm[:, :], power[:, :], ALU.pow).then_inc(rms_done, 1)

            def ln_power(i, g):
                pool.wait_ge(vare_done, g * 2 + i + 1)
                tt(rstd[:, i, :], vare[:, i, :], power[:, :], ALU.pow).then_inc(rstd_done, 1)

            def first_states(g):
                if not first(g):
                    pool.wait_ge(state_done, g * S)
                nc.gpsimd.tensor_copy(kv[:, :, :, 0], s0[:, bass.ds(g, 1), :, :].rearrange(
                    "p g s a -> p (g s) a")).then_inc(s0_done, 1)

            def add_xa(f, g):
                taken(pool, f"mix{f}", g)
                m = mixed[:, f, :, :].rearrange("p h (b l) -> p (h b) l", l=L)
                tt(m, m, xa[:, :, :, 1:L + 1].rearrange("p h b l -> p (h b) l"), add).then_inc(mixed_done, 1)

            def read_state(t, g):
                if t == 0:
                    taken(pool, "r", g)
                pool.wait_ge(state_done, g * S + t + 1)
                tt(rs[:, t % NR, :], r1[:, :, :, :].rearrange("p h b l -> p (h b l)"), state[:, t % NR, :],
                   mult).then_inc(rs_done, 1)

            def both(g0, g1, g2):
                a, b = g0 is not None, g1 is not None
                if b: ln_power(0, g1); first_states(g1)
                if a: residuals(g0)
                for n in range(NS + 1):
                    if b and n < MAA: add_xa(n, g1)
                    if a and n >= 1: normalise(n - 1, g0)
                if b: read_state(0, g1); read_state(1, g1); read_state(2, g1)
                if a: rms_power(g0)
                if b:
                    for t in range(3, S): read_state(t, g1)
                    ln_power(1, g1)

            pool.wait_ge(small_w, 16 * len(SMALL))
            pool.wait_ge(setup, SETUP)
            both(0, None, None)
            pool.wait_ge(l1_w, 16 * len(L1_LOADS))
            pool.wait_ge(l1_const, 2)
            both(1, 0, None)
            with pool.Fori(2, GROUPS) as i:
                both(i, i - 1, i - 2)
            both(None, GROUPS - 1, GROUPS - 2)
            both(None, None, GROUPS - 1)

        @blk.vector
        def _(dve):
            tt, ts, stt = nc.vector.tensor_tensor, nc.vector.tensor_scalar, nc.vector.scalar_tensor_tensor

            def v_out(g):
                for n in range(2):
                    full(dve, f"v{n}", g)
                    for j in range(2):
                        last = tt(v_z[:, 2 * n + j, :, 0:4:3, :],
                                  psum(f"v{n}")[:, j * C:(j + 1) * C].rearrange("p (r a d) -> p r a d", a=2, d=DH),
                                  rows[:, VB, :].rearrange("p (r a d) -> p r a d", a=2, d=DH), add)
                    freed(last, f"v{n}")

            def mask_row(g):
                dve.wait_ge(mask_in, g * 16 + 16)
                full(dve, "v1", g)
                ts(mask[:, :, 0:L], mask_i[:, :, :], 0, MASKED, ALU.is_equal, mult).then_inc(mask_done, 1)

            def row_max(n, g):
                full(dve, f"s{n}", g)
                nc.vector.tensor_reduce(nmax[:, n, :], psum(f"s{n}")[:, :].rearrange("p (j k) -> p j k", j=4),
                                        AX.X, amax, negate=True).then_inc(nmax_done, 1)

            def reciprocals(n, g):
                taken(dve, f"s{n}", g)
                nc.vector.reciprocal(rden[:, n, :], den[:, n, :]).then_inc(rden_done, 1)

            def probs_T(n, g):
                full(dve, f"p{n}", g)
                freed(nc.vector.tensor_copy(prob_T[:, n // R, n % R, :, :],
                                            psum(f"p{n}")[:, :].rearrange("p (j q) -> p j q", j=4)), f"p{n}")

            def att_out(bp, g):
                full(dve, f"o{bp}", g)
                freed(nc.vector.tensor_copy(att_T[:, :, bp * P:(bp + 1) * P],
                                            psum(f"o{bp}")[:, 0:H * P].rearrange("p (h q) -> p h q", h=H)), f"o{bp}")

            def residual(use, dst, x, x_done, g):
                if x_done is not None:
                    dve.wait_ge(x_done, g + 1)
                full(dve, use, g)
                freed(tt(dst[:, :, :], psum(use)[:, :].rearrange("p (t c) -> p t c", t=TT), x[:, :, :], add), use)

            def rms_mean(g):
                dve.wait_ge(ss_done, g + 1)
                ts(ssm[:, :], ss[:, :], 1.0 / C, EPS0, mult, add).then_inc(ssm_done, 1)

            def rms_norm(g):
                dve.wait_ge(rms_done, g + 1)
                taken(dve, "out", g)
                for t in range(TT):
                    last = ts(nrm[:, t, :], res[:, t, :], rms[:, t:t + 1], None, mult)
                last.then_inc(nrm_done, 1)

            def ln_stats(i, x, x_use, g):
                taken(dve, x_use, g)
                for t in range(TT):
                    last = nc.vector.bn_stats(stats[:, i, t, :], x[:, t, :])
                last.then_inc(stat_done, 1)
                dve.wait_ge(stat_done, g * 2 + i + 1)
                nc.vector.memset(carrier[:, :], 0.0)
                for t in range(TT):
                    last = nc.vector.bn_aggr(mv[:, i, t, :], stats[:, i, t, :])
                last.then_inc(mv_done, 1)
                dve.wait_ge(mv_done, g * 2 + i + 1)
                ts(vare[:, i, :], mv[:, i, :, 1], EPS1, None, add).then_inc(vare_done, 1)

            def ln_norm(i, x, dst, g):
                dve.wait_ge(rstd_done, g * 2 + i + 1)
                for t in range(TT):
                    last = ts(dst[:, t, :], x[:, t, :], mv[:, i, t, 0:1], rstd[:, i, t:t + 1], sub, mult)
                last.then_inc(xh_done, 1)

            def shifted(i, use, x, d, w, bias, g):
                full(dve, use, g)
                nc.vector.tensor_copy(x[:, :, :, 0].rearrange("p h b -> p (h b)"),
                                      edge[:, bass.ds(g, 1), 1 - i, :].rearrange("p g a -> p (g a)")
                                      ).then_inc(edge_done, 1)
                for h in range(H):
                    last = ts(x[:, h, :, 1:L + 1], seqs(psum(use)[:, h * T:(h + 1) * T]), cols[:, w, h:h + 1],
                              cols[:, bias, h:h + 1], mult, add)
                freed(last, use)
                dve.wait_ge(edge_done, g * 2 + i + 1)
                taken(dve, use, g)
                tt(d[:, :, :, :].rearrange("p h b l -> p (h b) l"),
                   x[:, :, :, 0:L].rearrange("p h b l -> p (h b) l"),
                   x[:, :, :, 1:L + 1].rearrange("p h b l -> p (h b) l"), sub).then_inc(sx_done, 1)
                dve.wait_ge(sx_done, g * 2 + i + 1)

            def lerp(dst, x, d, col, h):
                return stt(seqs(dst[:, h, :]), d[:, h, :, :], cols[:, col, h:h + 1], x[:, h, :, 1:L + 1], mult, add)

            def maa_in(g):
                for h in range(H):
                    last = lerp(xx, xa, sx, MAAX, h)
                last.then_inc(xx_done, 1)

            def mix_m(f, g):
                full(dve, f"mix{f}", g)
                for h in range(H):
                    last = stt(mixed[:, f, h, :], psum(f"mix{f}")[:, h * T:(h + 1) * T], cols[:, MAA0 + f, h:h + 1],
                               sx[:, h, :, :].rearrange("p b l -> p (b l)"), add, mult)
                freed(last, f"mix{f}")

            def v_low(g):
                dve.wait_ge(vhi_done, g + 1)
                freed(tt(v_lo[:, :], psum("v")[:, :], v_hi[:, :].bitcast(f32), sub), "v")

            def gate_out(g):
                dve.wait_ge(tg_done, g + 1)
                freed(stt(gate[:, :, :].rearrange("p h t -> p (h t)"), gate[:, :, :].rearrange("p h t -> p (h t)"),
                          1.0, psum("g")[:, :], add, mult), "g")

            def r_u_k(g):
                taken(dve, "r", g)
                for h in range(H):
                    last = stt(ruk[:, h, :], k1[:, h, :, :].rearrange("p b l -> p (b l)"), cols[:, U, h:h + 1],
                               r1[:, h, :, :].rearrange("p b l -> p (b l)"), mult, mult)
                last.then_inc(ruk_done, 1)

            def bonus_out(g):
                taken(dve, "vc", g)
                full(dve, "bonus", g)
                freed(tt(bonus[:, :], psum("bonus")[:, :], v_c[:, :], mult), "bonus")

            def scan(t, g):
                full(dve, f"vr{t}", g)
                if t == 0:
                    dve.wait_ge(w_done, g + 1)
                    dve.wait_ge(s0_done, g + 1)
                freed(tt(kv[:, t, :, 1:L], k1[:, :, :, 0:L - 1].rearrange("p h b l -> p (h b) l"),
                         psum(f"vr{t}")[:, :].rearrange("p (a l) -> p a l", l=L)[:, :, 0:L - 1], mult), f"vr{t}")
                if not first(g) or t >= NR:
                    dve.wait_ge(rs_done, g * S + (t - NR + 1 if t >= NR else 0))
                taken(dve, f"vr{t}", g)
                nc.vector.tensor_tensor_scan(state[:, t % NR, :], w_sh[:, :, :, :].rearrange("p h b l -> p (h b l)"),
                                             kv[:, t, :, :].rearrange("p a l -> p (a l)"), 0.0, mult,
                                             add).then_inc(state_done, 1)

            def y_out(g):
                full(dve, "y", g)
                taken(dve, "bonus", g)
                freed(tt(yc[:, :, :].rearrange("p h t -> p (h t)"), psum("y")[:, :], bonus[:, :], add), "y")

            def var_out(g):
                full(dve, "var", g)
                freed(ts(gv[:, :], psum("var")[:, 0:TT * NH1], EPS1, None, add), "var")

            def widen(g):
                taken(dve, "var", g)
                ts(g_rstd[:, :].bitcast(i32), gv[:, :].bitcast(i32), -0.5, float(0x5f3759df), mult,
                   add).then_inc(newton_done, 1)
                for n in range(3):
                    k = g * 10 + 3 * n
                    dve.wait_ge(newton_done, k + 1)
                    tt(g_t[:, :], g_rstd[:, :], g_rstd[:, :], mult).then_inc(newton_done, 1)
                    dve.wait_ge(newton_done, k + 2)
                    stt(g_t[:, :], g_t[:, :], -0.5, gv[:, :], mult, mult).then_inc(newton_done, 1)
                    dve.wait_ge(newton_done, k + 3)
                    stt(g_rstd[:, :], g_t[:, :], 1.5, g_rstd[:, :], add, mult).then_inc(newton_done, 1)
                dve.wait_ge(newton_done, g * 10 + 10)
                nc.vector.tensor_copy(g_wide[:, :, :].rearrange("p t (n s) -> p (t n) s", s=S),
                                      g_rstd[:, :].unsqueeze(2).broadcast_to([P, TT * NH1, S])
                                      ).then_inc(gwide_done, 1)

            def group_norm(g):
                full(dve, "rstd", g)
                freed(tt(z[:, :, :].rearrange("p h t -> p (h t)"), psum("rstd")[:, :],
                         yc[:, :, :].rearrange("p h t -> p (h t)"), mult), "rstd")
                taken(dve, "rstd", g)
                for h in range(H):
                    last = ts(z[:, h, :], z[:, h, :], gn_half[:, 0, h:h + 1], gn_half[:, 1, h:h + 1], mult, add)
                last.then_inc(z2_done, 1)
                dve.wait_ge(z2_done, g + 1)
                taken(dve, "g", g)
                tt(z[:, :, :], z[:, :, :], gate[:, :, :], mult).then_inc(z_done, 1)

            def ffn_in(g):
                for dst, col in ((xk2, FMK), (xr2, FMR)):
                    for h in range(H):
                        last = lerp(dst, xa, sx, col, h)
                last.then_inc(xkr_done, 1)

            def out(g):
                full(dve, "fv", g)
                taken(dve, "fr", g)
                freed(stt(tr[:, :, :].rearrange("p t c -> p (t c)"), tr[:, :, :].rearrange("p t c -> p (t c)"), 1.0,
                          psum("fv")[:, :], add, mult), "fv")
                if not first(g):
                    dve.wait_ge(out_done, g * 16)
                taken(dve, "fv", g)
                stt(o[:, :, :], tr[:, :, :], 0.5, x2[:, :, :], mult, add).then_inc(o_done, 1)

            def both(g0, g1, g2):
                a, b, c = (g is not None for g in (g0, g1, g2))
                if c:
                    shifted(1, "xc", xa, sx, LN2W, LN2B, g2)
                    ffn_in(g2)
                if b:
                    ln_norm(0, x1, xh, g1)
                    shifted(0, "xa", xa, sx, LN1W, LN1B, g1)
                    maa_in(g1)
                if a: v_out(g0); mask_row(g0)
                if c: out(g2)
                for n in range(NS + 3):
                    if a and n < NS: row_max(n, g0)
                    if b and n < MAA: mix_m(n, g1)
                    if a and 1 <= n <= NS: reciprocals(n - 1, g0)
                    if b and n == 5: v_low(g1)
                    if b and n == 8: gate_out(g1); r_u_k(g1)
                    if a and n >= 3 and n % 2 == 0: probs_T(n - 3, g0)
                    if a and n == 8: att_out(0, g0)
                if b: bonus_out(g1); scan(0, g1); scan(1, g1)
                if a: att_out(1, g0)
                if b: scan(2, g1)
                if a: residual("out", res, x_ob, xob_done, g0)
                if b: scan(3, g1)
                if a: rms_mean(g0)
                if b: scan(4, g1)
                if a: rms_norm(g0)
                if b:
                    for t in range(5, S): scan(t, g1)
                    y_out(g1)
                    var_out(g1)
                    widen(g1)
                    group_norm(g1)
                    if not first(g1):
                        dve.wait_ge(o_done, g1)
                    residual("wo", x2, x1, None, g1)
                    ln_stats(1, x2, "wo", g1)
                    ln_norm(1, x2, xh2, g1)
                if a:
                    if b: taken(dve, "wo", g1)
                    residual("mlp", x1, x_b2, xb2_done, g0)
                    ln_stats(0, x1, "mlp", g0)

            nc.vector.memset(w_sh[:, :, :, 0], 0.0).then_inc(setup, 1)
            nc.vector.memset(v_z[:, :, :, :, :], 0.0).then_inc(setup, 1)
            nc.vector.memset(mask[:, :, L:KEYS], 0.0).then_inc(setup, 1)
            nc.vector.memset(ones[:, :], 1.0).then_inc(setup, 1)
            nc.vector.memset(power[:, :], -0.5).then_inc(setup, 1)
            dve.wait_ge(small_w, 16 * len(SMALL))
            ts(gn_half[:, :, :], cols[:, GNW:GNB + 1, :], 0.5, None, mult).then_inc(setup, 1)
            for par in range(2):
                last = ts(q_bias[:, :, par], cols[:, QB, :], parity[:, par:par + 1], None, mult)
            last.then_inc(setup, 1)
            dve.wait_ge(setup, SETUP)
            both(0, None, None)
            dve.wait_ge(l1_w, 16 * len(L1_LOADS))
            nc.vector.tensor_copy(rep[:, :, :], kv[:, 0:2, :, :].rearrange("p s a l -> p (s a l)")
                                  .rearrange("p (t m) -> p t m", t=S)).then_inc(l1_const, 1)
            nc.vector.tensor_copy(centre[:, :], kv[:, 2, 0:2, :].rearrange("p a l -> p (a l)")).then_inc(l1_const, 1)
            both(1, 0, None)
            with dve.Fori(2, GROUPS) as i:
                both(i, i - 1, i - 2)
            both(None, GROUPS - 1, GROUPS - 2)
            both(None, None, GROUPS - 1)


def shape_constants():
    p = np.arange(P)
    same = (p[:, None] // S == p[None, :] // S).astype(np.float32)
    at = (p[None, :] % S == np.arange(S)[:, None]).astype(np.float32)
    return {
        "ident": np.eye(P, dtype=np.float32),
        "block": same,
        "centre": np.eye(P, dtype=np.float32) - same / S,
        "mean16": np.ascontiguousarray((p[:, None] // S == np.arange(P // S)[None, :]).astype(np.float32) / S),
        "rep": np.ascontiguousarray((same[:, None, :] * at.T[:, :, None]).astype(np.float32)),
        "fold": np.ascontiguousarray((same[:, None, :] * (at[None, :, :] - 1 / S)).astype(np.float32)),
        "parity": np.stack([(p // DH % 2 == i).astype(np.float32) / DH for i in range(2)], axis=1),
    }


def kernel(**inputs):
    import concourse.bacc as bacc
    from concourse.bass_utils import run_bass_kernel_spmd

    a = {k: np.asarray(v) for k, v in inputs.items()}
    l0 = {k[len("L0_xattn_"):]: v for k, v in a.items() if k.startswith("L0_xattn_")}
    l1 = {k[len("L1_xattn_"):]: v for k, v in a.items() if k.startswith("L1_xattn_")}

    def rows_of(w):
        return np.ascontiguousarray(w.reshape(-1, P, w.shape[1]).transpose(1, 0, 2))

    def half_cols(v):
        return np.ascontiguousarray(v.reshape(-1, H, P).transpose(2, 0, 1))

    x, ctx = a["x"], a["ctx_2048"]
    h = np.concatenate([ctx, x], axis=1)
    h_T = h.reshape(GROUPS, GB, KEYS, H, P).transpose(0, 4, 3, 1, 2)
    vectors = [l0["q_b"], l0["kv_b"][0::2], l0["postnorm_w"], l1["ln1_w"], l1["ln1_b"], l1["ln2_w"], l1["ln2_b"],
               l1["maa_x"], l1["maa_w"], l1["maa_k"], l1["maa_v"], l1["maa_r"], l1["maa_g"], l1["time_decay"],
               l1["faaaa"].reshape(C), l1["gn_w"], l1["gn_b"], l1["fmaa_k"], l1["fmaa_r"]]
    s0 = ctx[:, 2:2 + S, :].reshape(GROUPS, GB, H, P, S).transpose(3, 0, 4, 2, 1)
    edge = ctx[:, 0:2, :].reshape(GROUPS, GB, 2, H, P).transpose(4, 0, 2, 3, 1)
    arrays = {
        "x": np.ascontiguousarray(x.reshape(B * L, C)),
        "h_T": np.ascontiguousarray(h_T).reshape(GROUPS, P, H * GB * KEYS),
        "q_w": rows_of(l0["q_w"]), "k_w": rows_of(l0["kv_w"][:, 0::2]), "v_w": rows_of(l0["kv_w"][:, 1::2]),
        "out_w": rows_of(l0["out_w"]), "w1": rows_of(l0["mlp_w1"]), "w2": rows_of(l0["mlp_w2"]),
        "b1": np.ascontiguousarray(l0["mlp_b1"].reshape(FC, P).T),
        "rows": np.ascontiguousarray(np.broadcast_to(
            np.stack([l0["kv_b"][1::2], l0["out_b"], l0["mlp_b2"]])[None], (P, 3, C))),
        "cols": half_cols(np.stack(vectors)),
        "mask": np.ascontiguousarray(a["mask_BxS2_ik0"]).reshape(1, B, L),
        "maa_w1": rows_of(l1["maa_w1"]),
        "maa_w2": np.ascontiguousarray(l1["maa_w2"][0:4].reshape(P, C)),
        "maa_w2g": np.ascontiguousarray(l1["maa_w2"][4]),
        "decay_w1": rows_of(l1["decay_w1"]), "decay_w2": l1["decay_w2"],
        "wr": rows_of(l1["Wr"].T), "wk": rows_of(l1["Wk"].T), "wv": rows_of(l1["Wv"].T), "wg": rows_of(l1["Wg"].T),
        "wo": rows_of(l1["Wo"].T), "fwk": rows_of(l1["fWk"].T), "fwr": rows_of(l1["fWr"].T),
        "fwv": rows_of(l1["fWv"].T),
        "s0": np.ascontiguousarray(s0).reshape(P, GROUPS, S, H * GB),
        "edge": np.ascontiguousarray(edge).reshape(P, GROUPS, 2, H * GB),
        **shape_constants(),
    }
    nc = bacc.Bacc("TRN2", target_bir_lowering=False, num_devices=1)
    io = {n: nc.dram_tensor(f"in_{n}", v.shape, mybir.dt.from_np(v.dtype), kind="ExternalInput").ap()
          for n, v in arrays.items()}
    io["out"] = nc.dram_tensor("out", (B * L, C), mybir.dt.float32, kind="ExternalOutput").ap()
    build(nc, io)
    r = run_bass_kernel_spmd(nc, [{f"in_{n}": v for n, v in arrays.items()}], core_ids=[0])
    return r.results[0]["out"].reshape(B, L, C)
```

```python
from contextlib import ExitStack

import numpy as np

import concourse.bass as bass
from concourse import mybir

B, L, C = 32, 64, 256
KEYS = 2 * L
NH0, DH = 16, 16
NH1, S = 32, 8
F = 4 * C
MAA = 5
DM, DD = 32, 64
P = 128
H = C // P
GB = 4
T = GB * L
TT = T // P
GROUPS = B // GB
R = 4
NS = (GB // 2) * R
FC = F // P
EPS0, EPS1 = 1e-6, 1e-5
MASKED = -1e30

BANK_USES = [
    ["q", "s1", "s3", "s5", "s7", "out", "m2"],
    ["k0", "s0", "s2", "s4", "s6", "norm", "m3"],
    ["k1", "v1", "p0", "p2", "p4", "p5", "p7", "m0", "mlp0"],
    ["v0", "p1", "p3", "o0", "p6", "o1", "m1", "mlp1"],
    ["xa", "mix1", "mix0", "r", "vr0", "vr3", "vr6"],
    ["maa", "mix3", "k", "decay1", "vc", "vr1", "vr4", "vr7"],
    ["mix2", "v", "mix4", "decay2", "bonus", "vr2", "vr5", "yc", "var", "rstd"],
    ["g", "y", "wo", "xc", "fk", "fr", "fv"],
]
BANK_OF = {use: (b, k, len(uses)) for b, uses in enumerate(BANK_USES) for k, use in enumerate(uses)}
MIX_ORDER = (2, 1, 3, 0, 4)
SETUP = 7
L1_CONST = 4


def build(nc, io):
    f32, f32r = mybir.dt.float32, mybir.dt.float32r
    bf16, i32 = mybir.dt.bfloat16, mybir.dt.int32
    ALU, ACT, AX = mybir.AluOpType, mybir.ActivationFunctionType, mybir.AxisListType
    mult, add, sub, amax = ALU.mult, ALU.add, ALU.subtract, ALU.max

    with ExitStack() as ctx:
        def sb(name, shape, dt=f32):
            return ctx.enter_context(nc.sbuf_tensor(name, shape, dt))

        def seqs_of_halves(t):
            return t[:, :, :].rearrange("p h (b l) -> p h b l", l=L)

        def sem(name):
            return ctx.enter_context(nc.semaphore(name))

        qkv_hi, qkv_lo = sb("qkv_hi", [P, 3, H, C], f32r), sb("qkv_lo", [P, 3, H, C], f32r)
        out_w = sb("out_w", [P, H, C])
        w1_hi, w1_lo = sb("w1_hi", [P, H, F], f32r), sb("w1_lo", [P, H, F], f32r)
        w2 = sb("w2", [P, FC, C])
        maa_w1 = sb("maa_w1", [P, H, MAA * DM])
        maa_w2 = sb("maa_w2", [P, C])
        maa_w2g = sb("maa_w2g", [DM, C])
        decay_w1 = sb("decay_w1", [P, H, DD])
        decay_w2 = sb("decay_w2", [DD, C])
        wr, wk, wv, wo, fwk, fwv = (sb(n, [P, H, C]) for n in ("wr", "wk", "wv", "wo", "fwk", "fwv"))
        wg_hi, wg_lo, fwr_hi, fwr_lo = (sb(n, [P, H, C], f32r) for n in ("wg_hi", "wg_lo", "fwr_hi", "fwr_lo"))
        cols = sb("cols", [P, 19, H])
        (QB, KB, POST, LN1W, LN1B, LN2W, LN2B, MAAX, MAA0, TD, U, GNW, GNB, FMK, FMR) = (
            0, 1, 2, 3, 4, 5, 6, 7, 8, 13, 14, 15, 16, 17, 18)
        b1 = sb("b1", [P, FC])
        rows = sb("rows", [P, 3, C])
        VB, OB, B2 = 0, 1, 2
        ident = sb("ident", [P, P])
        block = sb("block", [P, P])
        centre = sb("centre", [P, P], f32r)
        mean16 = sb("mean16", [P, P // S])
        rep = sb("rep", [P, S, P], f32r)
        head_sum = sb("head_sum", [P, 2, 32])
        to_heads = sb("to_heads", [P, P])
        parity = sb("parity", [P, 2])
        q_bias = sb("q_bias", [P, H, 2])
        gn_half = sb("gn_half", [P, 2, H])
        power = sb("power", [P, TT])
        ones = sb("ones", [P, P], bf16)
        table = sb("table", [1, 1])
        mask_i = sb("mask_i", [P, GB, L], i32)
        mask = sb("mask", [P, GB, KEYS], bf16)
        s0 = sb("s0", [P, GROUPS, S, H * GB])
        edge = sb("edge", [P, GROUPS, 2, H * GB])

        kv = sb("kv", [P, S, H * GB, L])
        h_T = sb("h_T", [P, H, GB, KEYS])
        h_hi, h_lo = (sb(n, [P, H, GB, KEYS], f32r) for n in ("h_hi", "h_lo"))
        x_tok = sb("x_tok", [P, TT, C])
        x_ob = x_tok
        x1 = sb("x1", [P, 2, TT, C])
        q_T = sb("q_T", [P, H, GB, 2, L])
        k_T = sb("k_T", [P, H, GB, KEYS])
        v_z = sb("v_z", [P, GB, H * R, 4, DH])
        nmax = sb("nmax", [P, NS, 4])
        den = sb("den", [P, NS, 4])
        rden = sb("rden", [P, NS, 4])
        prob = sb("prob", [P, 4, 4, KEYS])
        prob_T = sb("prob_T", [P, GB // 2, R, 4, P])
        att_T = sb("att_T", [P, H, T])
        nrm, res = (prob[:, i, :, :].rearrange("p j (a c) -> p (j a) c", a=1).rearrange(
            "p (t m) c -> p t (m c)", t=TT) for i in (0, 1))
        n_hi, n_lo = sb("n_hi", [P, H, T], f32r), sb("n_lo", [P, H, T], f32r)
        ss, ssm, rms = sb("ss", [P, TT]), sb("ssm", [P, TT]), sb("rms", [P, TT])
        hid = prob_T[:, :, :, :, :].rearrange("p b r j q -> p (b r j q)").rearrange("p (c t) -> p c t", t=T)
        x2 = sb("x2", [P, TT, C])
        stats = sb("stats", [P, 2, TT, 6])
        carrier = sb("carrier", [1, 1])
        mv = sb("mv", [P, 2, TT, 2])
        vare, rstd = sb("vare", [P, 2, TT]), sb("rstd_ln", [P, 2, TT])
        xh, xh2 = sb("xh", [P, TT, C]), sb("xh2", [P, TT, C])
        xa, xc = sb("xa", [P, H, GB, L + 1]), sb("xc", [P, H, GB, L + 1])
        sx = sb("sx", [P, H, GB, L])
        g_wide = xc[:, :, :, :].rearrange("p h b l -> p (h b l)")[:, 0:TT * C].rearrange("p (t c) -> p t c", t=TT)
        th, thg = sb("th", [P, T]), sb("thg", [DM, T])
        mixed_g = sb("mixed_g", [P, H, T])
        mixed = [kv[:, S - MAA + MIX_ORDER.index(f), :, :].rearrange("p (h b) l -> p h (b l)", h=H)
                 for f in range(MAA - 1)] + [mixed_g]
        d1 = sb("d1", [DD, T])
        w_sh = sb("w_sh", [P, H, GB, L])
        k1, r1 = sb("k1", [P, H, GB, L]), sb("r1", [P, H, GB, L])
        v_hi, v_lo = sb("v_hi", [P, H * T], f32r), sb("v_lo", [P, H * T], f32r)
        part_hi, part_lo = sb("part_hi", [P, H, T], f32r), sb("part_lo", [P, H, T], f32r)
        gate = sb("gate", [P, H, T])
        ew = gate[:, :, :].rearrange("p h (b l) -> p h b l", l=L)
        v_c = sb("v_c", [P, H * T])
        ruk, bonus = sb("ruk", [P, H, T]), sb("bonus", [P, H * T])
        xx = bonus[:, :].rearrange("p (h t) -> p h t", h=H)
        yc = sb("yc", [P, H, T])
        y_rows = yc
        sq = ruk
        gv, g_rstd, g_t = (sb(n, [P, TT * NH1]) for n in ("gv", "g_rstd", "g_t"))
        z = sb("z", [P, H, T])
        xk2, xr2 = sb("xk2", [P, H, T]), sb("xr2", [P, H, T])
        sc = seqs_of_halves(xr2)
        kk = z
        tr, o = xh2, sb("o", [P, TT, C])

        bank = [ctx.enter_context(nc.psum_tensor(f"bank{b}", [P, 512], f32)) for b in range(8)]
        bank_full = [sem(f"bank_full{b}") for b in range(8)]
        bank_free = [sem(f"bank_free{b}") for b in range(8)]

        def psum(use):
            return bank[BANK_OF[use][0]]

        def first(g):
            return isinstance(g, int) and g == 0

        def final(g):
            return isinstance(g, int) and g == GROUPS - 1

        def full(eng, use, g):
            b, k, n = BANK_OF[use]
            eng.wait_ge(bank_full[b], g * n + (k + 1))

        def room(eng, use, g):
            b, k, n = BANK_OF[use]
            if not first(g) or k:
                eng.wait_ge(bank_free[b], g * n + k)

        def taken(eng, use, g):
            b, k, n = BANK_OF[use]
            eng.wait_ge(bank_free[b], g * n + (k + 1))

        def filled(ins, use):
            ins.then_inc(bank_full[BANK_OF[use][0]], 1)

        def freed(ins, use):
            ins.then_inc(bank_free[BANK_OF[use][0]], 1)

        w1_in, w1_hi_done, w1_split, nhi_done = (sem(n) for n in ("w1_in", "w1_hi_done", "w1_split", "nhi_done"))
        qkv_hi_done, qkv_lo_done = sem("qkv_hi_done"), sem("qkv_lo_done")
        hhi_done, hlo_done = sem("hhi_done"), sem("hlo_done")
        q_w_in, kv_w_in, l0_w, l1_w, small_w = (sem(n) for n in ("q_w_in", "kv_w_in", "l0_w", "l1_w", "small_w"))
        mask_in, mask_done = sem("mask_in"), sem("mask_done")
        h_in, x_in, out_done = sem("h_in"), sem("x_in"), sem("out_done")
        setup = sem("setup")
        nmax_done = sem("nmax_done")
        rden_done = sem("rden_done")
        prob_done = sem("prob_done")
        xob_done, xb2_done = sem("xob_done"), sem("xb2_done")
        ss_done, ssm_done, rms_done, nrm_done = sem("ss_done"), sem("ssm_done"), sem("rms_done"), sem("nrm_done")
        stat_done, mv_done, vare_done, rstd_done, xh_done, edge_done, sx_done = (
            [sem(f"{n}{i + 1}_done") for i in range(2)] for n in ("stat", "mv", "vare", "rstd", "xh", "edge", "sx"))
        xx_done = sem("xx_done")
        mixed_done = sem("mixed_done")
        w_done, tg_done, ruk_done = sem("w_done"), sem("tg_done"), sem("ruk_done")
        s0_done, state_done, rs_done = sem("s0_done"), sem("state_done"), sem("rs_done")
        sq_done, newton_done, gwide_done = sem("sq_done"), sem("newton_done"), sem("gwide_done")
        z2_done, z_done = sem("z2_done"), sem("z_done")
        vhi_done, l1_const = sem("vhi_done"), sem("l1_const")
        w_hi_done = sem("w_hi_done")
        xr_hi_done, xr_lo_done, mg_hi_done, mg_lo_done = (
            sem(n) for n in ("xr_hi_done", "xr_lo_done", "mg_hi_done", "mg_lo_done"))
        xkr_done, kk_done, o_done = sem("xkr_done"), sem("kk_done"), sem("o_done")

        def seqs(ap):
            return ap.rearrange("p (a l) -> p a l", l=L)

        blk = ctx.enter_context(nc.Block())

        w1_parts = [(x, k, m) for x, (k, m) in zip((ruk, yc, z, xx), ((0, 0), (0, 1), (1, 0), (1, 1)))]
        qkv_w = [kv[:, 3 + i, :, :].rearrange("p a l -> p (a l)") for i in range(3)]
        wg_in, fwr_in = (kv[:, 6 + i, :, :].rearrange("p (k b) l -> p k (b l)", k=H) for i in range(2))
        L0_LATER = [(ident, "ident"), (out_w, "out_w"), (w2, "w2")]
        SMALL = [(b1, "b1"), (rows, "rows"), (cols, "cols"), (parity, "parity")]
        L1_LOADS = [(maa_w1, "maa_w1"), (maa_w2, "maa_w2"), (maa_w2g, "maa_w2g"), (decay_w1, "decay_w1"),
                    (decay_w2, "decay_w2"), (wr, "wr"), (wk, "wk"), (wv, "wv"), (wg_in, "wg"), (wo, "wo"),
                    (fwk, "fwk"), (fwr_in, "fwr"), (fwv, "fwv"), (block, "block"), (mean16, "mean16"),
                    (head_sum, "head_sum"), (to_heads, "to_heads"),
                    (kv[:, 0:2, :, :].rearrange("p s a l -> p (s a l)"), "rep"),
                    (kv[:, 2, 0:2, :].rearrange("p a l -> p (a l)"), "centre"), (s0, "s0"), (edge, "edge")]

        @blk.sync
        def _(sp):
            def load_h(g):
                if not first(g):
                    sp.wait_ge(hlo_done, g)
                sp.dma_start(h_T[:, :, :, :], io["h_T"][bass.ds(g, 1), :, :].rearrange(
                    "g p (h b k) -> p (g h) b k", h=H, b=GB)).then_inc(h_in, 16)

            def load_mask(g):
                if not first(g):
                    sp.wait_ge(mask_done, g)
                sp.dma_start(mask_i[:, :, :], io["mask"][:, bass.ds(g * GB, GB), :].broadcast_to(
                    [P, GB, L])).then_inc(mask_in, 16)

            def load_x(g):
                if not first(g):
                    taken(sp, "out", g - 1)
                sp.dma_start(x_tok[:, :, :], io["x"][bass.ds(g * T, T), :].rearrange(
                    "(t p) c -> p t c", p=P)).then_inc(x_in, 16)

            def store(g):
                sp.wait_ge(o_done, g + 1)
                sp.dma_start(io["out"][bass.ds(g * T, T), :].rearrange("(t p) c -> p t c", p=P),
                             o[:, :, :]).then_inc(out_done, 16)

            sp.dma_start(qkv_w[0], io["q_w"].rearrange("p h c -> p (h c)")).then_inc(q_w_in, 16)
            load_h(0)
            for dst, name in zip(qkv_w[1:], ("k_w", "v_w")):
                sp.dma_start(dst, io[name].rearrange("p h c -> p (h c)")).then_inc(kv_w_in, 16)
            load_mask(0)
            load_x(0)
            for dst, name in L0_LATER:
                sp.dma_start(dst[:], io[name]).then_inc(l0_w, 16)
            for dst, k, m in w1_parts:
                sp.dma_start(dst[:, :, :].rearrange("p h t -> p (h t)"),
                             io["w1"][:, k, m * 2 * T:(m + 1) * 2 * T]).then_inc(w1_in, 16)
            for dst, name in L1_LOADS:
                sp.dma_start(dst[:], io[name]).then_inc(l1_w, 16)
            load_h(1)
            load_mask(1)
            load_x(1)
            load_h(2)
            with sp.Fori(2, GROUPS - 1) as i:
                load_mask(i)
                load_x(i)
                load_h(i + 1)
                store(i - 2)
            load_mask(GROUPS - 1)
            load_x(GROUPS - 1)
            for g in range(GROUPS - 3, GROUPS):
                store(g)
            sp.wait_ge(out_done, 16 * GROUPS)

        @blk.tensor
        def _(pe):
            mm = nc.tensor.matmul

            def project_T(use, w, x, g):
                room(pe, use, g)
                for m in range(H):
                    for k in range(H):
                        last = mm(psum(use)[:, m * T:(m + 1) * T], w[:, k, m * P:(m + 1) * P], x[:, k, :],
                                  start=k == 0, stop=k == H - 1)
                filled(last, use)

            def project_split(use, w_hi, w_lo, g):
                room(pe, use, g)
                parts = [(w, x, k) for w, x in ((w_hi, part_hi), (w_lo, part_hi), (w_hi, part_lo)) for k in range(H)]
                for m in range(H):
                    for i, (w, x, k) in enumerate(parts):
                        last = mm(psum(use)[:, m * T:(m + 1) * T], w[:, k, m * P:(m + 1) * P], x[:, k, :],
                                  start=i == 0, stop=i == len(parts) - 1)
                filled(last, use)

            def project_tok(use, x, w, g):
                room(pe, use, g)
                for t in range(TT):
                    for k in range(H):
                        last = mm(psum(use)[:, t * C:(t + 1) * C], x[:, k, t * P:(t + 1) * P], w[:, k, :],
                                  start=k == 0, stop=k == H - 1)
                filled(last, use)

            def turn(use, x, g):
                room(pe, use, g)
                for t in range(TT):
                    for h in range(H):
                        last = nc.tensor.transpose(psum(use)[:, h * T + t * P:h * T + (t + 1) * P],
                                                   x[:, t, h * P:(h + 1) * P], ident[:, :])
                filled(last, use)

            PARTS = [(w, h, k) for w, h in ((qkv_hi, h_hi), (qkv_lo, h_hi), (qkv_hi, h_lo)) for k in range(H)]

            def split_in(i, g):
                if first(g):
                    pe.wait_ge(qkv_lo_done, i + 1)
                pe.wait_ge(hlo_done, g + 1)

            def q_proj(g):
                split_in(0, g)
                room(pe, "q", g)
                for m in range(H):
                    for i, (w, h, k) in enumerate(PARTS):
                        last = mm(psum("q")[:, m * T:(m + 1) * T], w[:, 0, k, m * P:(m + 1) * P], h[:, k, :, L:KEYS],
                                  start=i == 0, stop=i == len(PARTS) - 1)
                filled(last, "q")

            def k_proj(m, g):
                split_in(1, g)
                room(pe, f"k{m}", g)
                for i, (w, h, k) in enumerate(PARTS):
                    last = mm(psum(f"k{m}")[:, :], w[:, 1, k, m * P:(m + 1) * P], h[:, k, :, :],
                              start=i == 0, stop=i == len(PARTS) - 1)
                filled(last, f"k{m}")

            def v_proj(n, g, seqs_of_bank=(0, 1)):
                split_in(2, g)
                if 0 in seqs_of_bank:
                    room(pe, f"v{n}", g)
                for j in seqs_of_bank:
                    for i, (w, h, k) in enumerate(PARTS):
                        last = mm(psum(f"v{n}")[:, j * C:(j + 1) * C], h[:, k, 2 * n + j, :], w[:, 2, k, :],
                                  start=i == 0, stop=i == len(PARTS) - 1)
                if 1 in seqs_of_bank:
                    filled(last, f"v{n}")

            def scores(n, g):
                bp, r = n // R, n % R
                if n == 0:
                    taken(pe, "q", g)
                    taken(pe, "k0", g)
                    taken(pe, "k1", g)
                    pe.wait_ge(mask_done, g + 1)
                    if first(g):
                        pe.wait_ge(setup, SETUP)
                room(pe, f"s{n}", g)
                out = psum(f"s{n}")
                for j in range(4):
                    b, h = 2 * bp + j // 2, j % 2
                    mm(out[:, j * P:(j + 1) * P], q_T[32 * r:32 * r + 32, h, b, :, :],
                       k_T[32 * r:32 * r + 32, h, b, :], start=j == 0, stop=False, skip_group_check=True)
                filled(mm(out[:, :], ones[32 * r:32 * r + 1, :], mask[32 * r:32 * r + 1, 2 * bp:2 * bp + 2, :]
                          .unsqueeze(2).broadcast_to([1, 2, H, KEYS]), start=False, stop=True,
                          skip_group_check=True), f"s{n}")

            def turn_probs(n, g):
                if first(g) and n == 0:
                    pe.wait_ge(l0_w, 16 * len(L0_LATER))
                pe.wait_ge(prob_done, g * NS + n + 1)
                room(pe, f"p{n}", g)
                for j in range(4):
                    last = nc.tensor.transpose(psum(f"p{n}")[:, j * P:(j + 1) * P], prob[:, n % 4, j, :], ident[:, :])
                filled(last, f"p{n}")

            def attend(bp, g):
                taken(pe, f"p{R * bp + 2}", g)
                taken(pe, f"p{R * bp + 3}", g)
                if bp:
                    taken(pe, "v1", g)
                room(pe, f"o{bp}", g)
                for j in range(4):
                    b, h = 2 * bp + j // 2, j % 2
                    c = h * P + (j // 2) * L
                    for par in range(2):
                        for r in range(R):
                            last = mm(psum(f"o{bp}")[32 * r:32 * r + 32, c:c + L],
                                      v_z[:, b, h * R + r, 2 * par:2 * par + 2, :],
                                      prob_T[:, bp, r, j, par * L:(par + 1) * L], start=par == 0, stop=par == 1)
                filled(last, f"o{bp}")

            def out_proj(g):
                taken(pe, "o1", g)
                project_tok("out", att_T, out_w, g)

            def turn_norm(g):
                pe.wait_ge(nrm_done, g + 1)
                turn("norm", nrm, g)

            def mlp_up(n, g):
                if n == 0:
                    if first(g): pe.wait_ge(w1_split, 1)
                    pe.wait_ge(nhi_done, g + 1)
                room(pe, f"m{n}", g)
                parts = [(w, x, k) for w, x in ((w1_hi, n_hi), (w1_lo, n_hi), (w1_hi, n_lo)) for k in range(H)]
                for i, (w, x, k) in enumerate(parts):
                    if n == 0 and i == 2 * H:
                        taken(pe, "norm", g)
                    for j in range(2):
                        c = (2 * n + j) * P
                        last = mm(psum(f"m{n}")[:, j * T:(j + 1) * T], w[:, k, c:c + P], x[:, k, :],
                                  start=i == 0 and j == 0, stop=i == len(parts) - 1, skip_group_check=True)
                filled(last, f"m{n}")

            def mlp_down(t, g, chunks=range(FC)):
                if 0 in chunks:
                    room(pe, f"mlp{t}", g)
                for k in chunks:
                    if t == 0 and k % 2 == 0:
                        taken(pe, f"m{k // 2}", g)
                    last = mm(psum(f"mlp{t}")[:, 0:C], hid[:, k, t * P:(t + 1) * P], w2[:, k, :],
                              start=k == 0, stop=k == FC - 1)
                if FC - 1 in chunks:
                    filled(last, f"mlp{t}")

            def turn_xa(g):
                pe.wait_ge(xh_done[0], g + 1)
                turn("xa", xh, g)

            def maa(g):
                pe.wait_ge(xx_done, g + 1)
                room(pe, "maa", g)
                for k in range(H):
                    mm(psum("maa")[:, 0:T], maa_w1[:, k, 0:P], xx[:, k, :], start=k == 0, stop=k == H - 1)
                for k in range(H):
                    last = mm(psum("maa")[0:DM, T:2 * T], maa_w1[:, k, P:P + DM], xx[:, k, :],
                              start=k == 0, stop=k == H - 1)
                filled(last, "maa")

            def mix(f, g):
                if f == MIX_ORDER[0]:
                    taken(pe, "maa", g)
                room(pe, f"mix{f}", g)
                for h in range(H):
                    if f < 4:
                        w, x = maa_w2[32 * f:32 * f + 32, h * P:(h + 1) * P], th[32 * f:32 * f + 32, :]
                    else:
                        w, x = maa_w2g[:, h * P:(h + 1) * P], thg[:, :]
                    last = mm(psum(f"mix{f}")[:, h * T:(h + 1) * T], w, x, start=True, stop=True)
                filled(last, f"mix{f}")

            def decay1(g):
                pe.wait_ge(mixed_done, g * MAA + MIX_ORDER.index(0) + 1)
                room(pe, "decay1", g)
                for k in range(H):
                    last = mm(psum("decay1")[0:DD, 0:T], decay_w1[:, k, :], mixed[0][:, k, :],
                              start=k == 0, stop=k == H - 1)
                filled(last, "decay1")

            def decay2(g):
                taken(pe, "decay1", g)
                room(pe, "decay2", g)
                for h in range(H):
                    last = mm(psum("decay2")[:, h * T:(h + 1) * T], decay_w2[:, h * P:(h + 1) * P], d1[:, :],
                              start=True, stop=True)
                filled(last, "decay2")

            def proj(use, f, w, g):
                pe.wait_ge(mixed_done, g * MAA + MIX_ORDER.index(f) + 1)
                project_T(use, w, mixed[f], g)

            def v_centred(g):
                taken(pe, "v", g)
                room(pe, "vc", g)
                mm(psum("vc")[:, :], centre[:, :], v_hi[:, :], start=True, stop=False)
                filled(mm(psum("vc")[:, :], centre[:, :], v_lo[:, :], start=False, stop=True), "vc")

            def bonus_sum(g):
                pe.wait_ge(ruk_done, g + 1)
                room(pe, "bonus", g)
                filled(mm(psum("bonus")[:, :], block[:, :], ruk[:, :, :], start=True, stop=True), "bonus")

            def v_rep(t, g):
                room(pe, f"vr{t}", g)
                mm(psum(f"vr{t}")[:, :], rep[:, t, :], v_hi[:, :], start=True, stop=False)
                filled(mm(psum(f"vr{t}")[:, :], rep[:, t, :], v_lo[:, :], start=False, stop=True), f"vr{t}")

            def y_sum(part, g):
                pe.wait_ge(rs_done, g * S + 4 * part + 4)
                if part == 0:
                    room(pe, "y", g)
                for i in range(4):
                    last = mm(psum("y")[32 * i:32 * i + 32, :], head_sum[:, part, :],
                              kv[:, 4 * part + i, :, :].rearrange("p a l -> p (a l)"),
                              start=part == 0, stop=part == 1)
                if part == 1:
                    filled(last, "y")

            def y_centred(g):
                taken(pe, "y", g)
                room(pe, "yc", g)
                filled(mm(psum("yc")[:, :], to_heads[:, :], y_rows[:, :, :].rearrange("p h t -> p (h t)"),
                          start=True, stop=True), "yc")

            def variance(g):
                pe.wait_ge(sq_done, g + 1)
                room(pe, "var", g)
                n = P // S
                for t in range(TT):
                    for h in range(H):
                        c = (t * H + h) * n
                        last = mm(psum("var")[:, c:c + n], sq[:, h, t * P:(t + 1) * P], mean16[:, :],
                                  start=True, stop=True)
                filled(last, "var")

            def turn_rstd(g):
                pe.wait_ge(gwide_done, g + 1)
                room(pe, "rstd", g)
                for t in range(TT):
                    for h in range(H):
                        last = nc.tensor.transpose(psum("rstd")[:, h * T + t * P:h * T + (t + 1) * P],
                                                   g_wide[:, t, h * P:(h + 1) * P], ident[:, :])
                filled(last, "rstd")

            def w_out(g):
                pe.wait_ge(z_done, g + 1)
                project_tok("wo", z, wo, g)

            def turn_xc(g):
                pe.wait_ge(xh_done[1], g + 1)
                turn("xc", xh2, g)

            def ffn_key(g):
                pe.wait_ge(xkr_done, g + 1)
                project_T("fk", fwk, xk2, g)

            def ffn_recept(g):
                pe.wait_ge(xr_lo_done, g + 1)
                room(pe, "fr", g)
                parts = [(x, w, k) for x, w in ((part_hi, fwr_hi), (part_hi, fwr_lo), (part_lo, fwr_hi))
                         for k in range(H)]
                for t in range(TT):
                    for i, (x, w, k) in enumerate(parts):
                        last = mm(psum("fr")[:, t * C:(t + 1) * C], x[:, k, t * P:(t + 1) * P], w[:, k, :],
                                  start=i == 0, stop=i == len(parts) - 1)
                filled(last, "fr")

            def gate_proj(g):
                pe.wait_ge(mg_lo_done, g + 1)
                project_split("g", wg_hi, wg_lo, g)

            def ffn_value(g):
                pe.wait_ge(kk_done, g + 1)
                project_tok("fv", kk, fwv, g)

            def both(g0, g1, g2):
                a, b, c = (g is not None for g in (g0, g1, g2))
                if a:
                    q_proj(g0)
                    k_proj(0, g0)
                    k_proj(1, g0)
                if b: turn_xa(g1)
                if a: v_proj(0, g0); v_proj(1, g0, [0])
                if c: turn_rstd(g2)
                if b:
                    if first(g1):
                        pe.wait_ge(l1_w, 16 * len(L1_LOADS))
                        pe.wait_ge(l1_const, L1_CONST)
                    maa(g1)
                for n in range(NS + 3):
                    if a and n < NS: scores(n, g0)
                    if b and n == 3: proj("k", 1, wk, g1)
                    if b and n == 4: proj("r", 3, wr, g1)
                    if b and n < MAA: mix(MIX_ORDER[n], g1)
                    if a and n == 0: v_proj(1, g0, [1])
                    if c and n == 1: w_out(g2)
                    if b and n == 2: proj("v", 2, wv, g1)
                    if b and n == 5: decay1(g1)
                    if a and n >= 3: turn_probs(n - 3, g0)
                    if c and n == 5: turn_xc(g2)
                    if b and n == 6: decay2(g1)
                    if b and n == 7: v_centred(g1)
                    if a and n == R + 3: attend(0, g0)
                    if c and n == 7: ffn_key(g2)
                    if b and n == 8: bonus_sum(g1); v_rep(0, g1)
                    if b and n == 9: v_rep(1, g1); v_rep(2, g1)
                    if b and n == 10: v_rep(3, g1)
                    if c and n == 10: ffn_recept(g2)
                if a: attend(1, g0)
                if b: v_rep(4, g1)
                if a: out_proj(g0)
                if b: v_rep(5, g1)
                if c: ffn_value(g2)
                if b: v_rep(6, g1); v_rep(7, g1)
                if a: turn_norm(g0)
                if b: gate_proj(g1)
                if a: mlp_up(0, g0); mlp_up(1, g0)
                if b: y_sum(0, g1)
                if a: mlp_up(2, g0); mlp_up(3, g0)
                if b: y_sum(1, g1)
                if a: mlp_down(0, g0, range(FC // 2))
                if b: y_centred(g1)
                if a: mlp_down(0, g0, range(FC // 2, FC))
                if b: variance(g1)
                if a: mlp_down(1, g0)

            both(0, None, None)
            both(1, 0, None)
            with pe.Fori(2, GROUPS - 2) as i:
                both(i, i - 1, i - 2)
            both(GROUPS - 2, GROUPS - 3, GROUPS - 4)
            both(GROUPS - 1, GROUPS - 2, GROUPS - 3)
            both(None, GROUPS - 1, GROUPS - 2)
            both(None, None, GROUPS - 1)

        @blk.scalar
        def _(act):
            fn = nc.scalar.activation

            def q_out(g):
                full(act, "q", g)
                for h in range(H):
                    for par in range(2):
                        last = fn(q_T[:, h, :, par, :], seqs(psum("q")[:, h * T:(h + 1) * T]), ACT.Identity,
                                  bias=q_bias[:, h, par:par + 1], scale=parity[:, par:par + 1])
                freed(last, "q")

            def k_out(m, g):
                full(act, f"k{m}", g)
                freed(fn(k_T[:, m, :, :], psum(f"k{m}")[:, :].rearrange("p (b k) -> p b k", b=GB),
                         ACT.Identity, bias=cols[:, KB, m:m + 1]), f"k{m}")

            def exps(n, g):
                act.wait_ge(nmax_done, g * NS + n + 1)
                for j in range(4):
                    last = fn(prob[:, n % 4, j, :], psum(f"s{n}")[:, j * P:(j + 1) * P], ACT.Exp,
                              bias=nmax[:, n, j:j + 1], accum_out=den[:, n, j:j + 1])
                freed(last, f"s{n}")

            def probs_T(n, g):
                if n == 0 and not first(g):
                    full(act, "mlp1", g - 1)
                full(act, f"p{n}", g)
                freed(fn(prob_T[:, n // R, n % R, :, :], psum(f"p{n}")[:, :].rearrange("p (j q) -> p j q", j=4),
                         ACT.Copy), f"p{n}")

            def squares(g):
                taken(act, "out", g)
                for t in range(TT):
                    last = fn(nrm[:, t, :], res[:, t, :], ACT.Square, accum_out=ss[:, t:t + 1])
                last.then_inc(ss_done, 1)

            def norm_T(g):
                full(act, "norm", g)
                for h in range(H):
                    last = fn(n_hi[:, h, :], psum("norm")[:, h * T:(h + 1) * T], ACT.Identity,
                              scale=cols[:, POST, h:h + 1])
                last.then_inc(nhi_done, 1)

            def gelu(n, g):
                full(act, f"m{n}", g)
                for j in range(2):
                    c = 2 * n + j
                    last = fn(hid[:, c, :], psum(f"m{n}")[:, j * T:(j + 1) * T], ACT.Gelu_apprx_tanh,
                              bias=b1[:, c:c + 1])
                freed(last, f"m{n}")

            def maa_tanh(g):
                full(act, "maa", g)
                fn(th[:, :], psum("maa")[:, 0:T], ACT.Tanh)
                freed(fn(thg[:, :], psum("maa")[0:DM, T:2 * T], ACT.Tanh), "maa")

            def decay_tanh(g):
                full(act, "decay1", g)
                freed(fn(d1[:, :], psum("decay1")[0:DD, 0:T], ACT.Tanh), "decay1")

            def decays(g):
                if not first(g):
                    act.wait_ge(z_done, g)
                full(act, "decay2", g)
                for h in range(H):
                    last = fn(ew[:, h, :, :], seqs(psum("decay2")[:, h * T:(h + 1) * T]), ACT.Exp,
                              bias=cols[:, TD, h:h + 1])
                freed(last, "decay2")
                taken(act, "decay2", g)
                fn(w_sh[:, :, :, 1:L].rearrange("p h b l -> p (h b) l"),
                   ew[:, :, :, 0:L - 1].rearrange("p h b l -> p (h b) l"), ACT.Exp, scale=-1.0).then_inc(w_done, 1)

            def keep(use, dst, g):
                full(act, use, g)
                freed(fn(dst, psum(use)[:, :], ACT.Copy), use)

            def v_high(g):
                full(act, "v", g)
                fn(v_hi[:, :], psum("v")[:, :], ACT.Copy).then_inc(vhi_done, 1)

            def gate_tanh(g):
                full(act, "g", g)
                act.wait_ge(w_done, g + 1)
                fn(gate[:, :, :], psum("g")[:, :], ACT.Tanh, scale=0.5).then_inc(tg_done, 1)

            def y_square(g):
                taken(act, "yc", g)
                fn(sq[:, :, :], yc[:, :, :], ACT.Square).then_inc(sq_done, 1)

            def relu_square(g):
                full(act, "fk", g)
                freed(fn(kk[:, :, :], psum("fk")[:, :], ACT.Relu), "fk")
                taken(act, "fk", g)
                fn(kk[:, :, :], kk[:, :, :], ACT.Square).then_inc(kk_done, 1)

            def xr_high(g):
                act.wait_ge(xkr_done, g + 1)
                full(act, "g", g)
                fn(part_hi[:, :, :], xr2[:, :, :], ACT.Copy).then_inc(xr_hi_done, 1)

            def mg_high(g):
                act.wait_ge(mixed_done, g * MAA + MIX_ORDER.index(4) + 1)
                if not first(g):
                    full(act, "fr", g - 1)
                fn(part_hi[:, :, :], mixed_g[:, :, :], ACT.Copy).then_inc(mg_hi_done, 1)

            def recept_tanh(g):
                full(act, "fr", g)
                freed(fn(tr[:, :, :], psum("fr")[:, :], ACT.Tanh, scale=0.5), "fr")

            def h_high(g):
                act.wait_ge(h_in, g * 16 + 16)
                if not first(g):
                    full(act, "v1", g - 1)
                for k in range(H):
                    last = fn(h_hi[:, k, :, :], h_T[:, k, :, :], ACT.Copy)
                last.then_inc(hhi_done, 1)

            def w1_high():
                act.wait_ge(w1_in, 16 * len(w1_parts))
                for x, k, m in w1_parts:
                    last = fn(w1_hi[:, k, m * 2 * T:(m + 1) * 2 * T], x[:, :, :].rearrange("p h t -> p (h t)"),
                              ACT.Copy)
                last.then_inc(w1_hi_done, 1)

            def exp_table():
                fn(table[:, :], power[0:1, 0:1], ACT.Exp)

            def both(g0, g1, g2):
                a, b, c = (g is not None for g in (g0, g1, g2))
                if a: q_out(g0); k_out(0, g0); k_out(1, g0)
                if b: maa_tanh(g1)
                for n in range(NS + 3):
                    if a and n < NS: exps(n, g0)
                    if b and n == 2: v_high(g1)
                    if b and n == 3: keep("k", k1[:, :, :, :], g1)
                    if b and n == 4: keep("r", r1[:, :, :, :], g1)
                    if b and n == 5: decay_tanh(g1)
                    if b and n == 7: keep("vc", v_c[:, :], g1)
                    if a and n >= 3 and n % 2: probs_T(n - 3, g0)
                    if a and n == 6 and not final(g0): h_high(g0 + 1)
                    if b and n == 7: decays(g1)
                    if c and n == 7: xr_high(g2); relu_square(g2)
                if b: mg_high(g1)
                if c: recept_tanh(g2)
                if a:
                    if first(g0): w1_high()
                    squares(g0)
                if a: norm_T(g0)
                if b: gate_tanh(g1)
                if a:
                    for n in range(FC // 2): gelu(n, g0)
                if b: keep("y", y_rows[:, :, :], g1)
                if b: y_square(g1)
                if a: exp_table()

            for dst, name in SMALL:
                act.dma_start(dst[:], io[name]).then_inc(small_w, 16)
            for i in range(3):
                act.wait_ge(kv_w_in if i else q_w_in, 32 if i else 16)
                fn(qkv_hi[:, i, :, :].rearrange("p h c -> p (h c)"), qkv_w[i], ACT.Copy).then_inc(qkv_hi_done, 1)
                if i == 0:
                    h_high(0)
            act.wait_ge(small_w, 16 * len(SMALL))
            act.wait_ge(setup, SETUP)
            both(0, None, None)
            both(1, 0, None)
            with act.Fori(2, GROUPS - 2) as i:
                both(i, i - 1, i - 2)
            both(GROUPS - 2, GROUPS - 3, GROUPS - 4)
            both(GROUPS - 1, GROUPS - 2, GROUPS - 3)
            both(None, GROUPS - 1, GROUPS - 2)
            both(None, None, GROUPS - 1)

        @blk.gpsimd
        def _(pool):
            tt = nc.gpsimd.tensor_tensor

            def residual_mlp(g, par):
                pool.wait_ge(x_in, g * 16 + 16)
                if not (isinstance(g, int) and g < 2):
                    taken(pool, "wo", g - 2)
                tt(x1[:, par, :, :], x_tok[:, :, :], rows[:, B2, :].unsqueeze(1).broadcast_to([P, TT, C]),
                   add).then_inc(xb2_done, 1)

            def residual_out(g):
                pool.wait_ge(xb2_done, g + 1)
                tt(x_ob[:, :, :], x_tok[:, :, :], rows[:, OB, :].unsqueeze(1).broadcast_to([P, TT, C]),
                   add).then_inc(xob_done, 1)

            def normalise(n, g):
                pool.wait_ge(rden_done, g * NS + n + 1)
                p = prob[:, n % 4, :, :]
                tt(p, p, rden[:, n, :].unsqueeze(2).broadcast_to([P, 4, KEYS]), mult).then_inc(prob_done, 1)

            def rms_power(g):
                pool.wait_ge(ssm_done, g + 1)
                tt(rms[:, :], ssm[:, :], power[:, :], ALU.pow).then_inc(rms_done, 1)

            def h_low(g):
                pool.wait_ge(hhi_done, g + 1)
                tt(h_lo[:, :, :, :], h_T[:, :, :, :], h_hi[:, :, :, :].bitcast(f32), sub).then_inc(hlo_done, 1)

            def ln_power(i, g):
                pool.wait_ge(vare_done[i], g + 1)
                tt(rstd[:, i, :], vare[:, i, :], power[:, :], ALU.pow).then_inc(rstd_done[i], 1)

            def first_states(g):
                if not first(g):
                    full(pool, "y", g - 1)
                full(pool, "decay1", g)
                nc.gpsimd.tensor_copy(kv[:, :, :, 0], s0[:, bass.ds(g, 1), :, :].rearrange(
                    "p g s a -> p (g s) a")).then_inc(s0_done, 1)

            def add_xa(f, g):
                taken(pool, f"mix{f}", g)
                m = mixed[f][:, :, :].rearrange("p h (b l) -> p (h b) l", l=L)
                tt(m, m, xa[:, :, :, 1:L + 1].rearrange("p h b l -> p (h b) l"), add).then_inc(mixed_done, 1)

            def xr_low(g):
                pool.wait_ge(xr_hi_done, g + 1)
                tt(part_lo[:, :, :], xr2[:, :, :], part_hi[:, :, :].bitcast(f32), sub).then_inc(xr_lo_done, 1)

            def mg_low(g):
                pool.wait_ge(mg_hi_done, g + 1)
                tt(part_lo[:, :, :], mixed_g[:, :, :], part_hi[:, :, :].bitcast(f32), sub).then_inc(mg_lo_done, 1)

            def read_state(t, g):
                if t == 0:
                    taken(pool, "r", g)
                pool.wait_ge(state_done, g * S + t + 1)
                states = kv[:, t, :, :]
                tt(states, r1[:, :, :, :].rearrange("p h b l -> p (h b) l"), states, mult).then_inc(rs_done, 1)

            def both(g0, g1, g2, par):
                a, b, c = (g is not None for g in (g0, g1, g2))
                for n in range(NS + 1):
                    if b and n < MAA: add_xa(MIX_ORDER[n], g1)
                    if a and n >= 1: normalise(n - 1, g0)
                    if c and n == 2: ln_power(1, g2)
                    if a and n == 5: residual_mlp(g0, par)
                    if a and n == 6: residual_out(g0)
                    if b and n == 7: first_states(g1)
                    if c and n == 8: xr_low(g2)
                    if a and n == 8 and not final(g0): h_low(g0 + 1)
                if b:
                    mg_low(g1)
                    for t in range(3): read_state(t, g1)
                if a: rms_power(g0)
                if b:
                    for t in range(3, S): read_state(t, g1)
                if a: ln_power(0, g0)

            h_low(0)
            pool.wait_ge(small_w, 16 * len(SMALL))
            pool.wait_ge(setup, SETUP)
            both(0, None, None, 0)
            pool.wait_ge(l1_w, 16 * len(L1_LOADS))
            pool.wait_ge(l1_const, L1_CONST)
            both(1, 0, None, 1)
            with pool.Fori(2, GROUPS - 2, 2) as i:
                both(i, i - 1, i - 2, 0)
                both(i + 1, i, i - 1, 1)
            both(GROUPS - 2, GROUPS - 3, GROUPS - 4, 0)
            both(GROUPS - 1, GROUPS - 2, GROUPS - 3, 1)
            both(None, GROUPS - 1, GROUPS - 2, 0)
            both(None, None, GROUPS - 1, 1)

        @blk.vector
        def _(dve):
            tt, ts, stt = nc.vector.tensor_tensor, nc.vector.tensor_scalar, nc.vector.scalar_tensor_tensor

            def v_out(n, g):
                full(dve, f"v{n}", g)
                for j in range(2):
                    last = tt(v_z[:, 2 * n + j, :, 0:4:3, :],
                              psum(f"v{n}")[:, j * C:(j + 1) * C].rearrange("p (r a d) -> p r a d", a=2, d=DH),
                              rows[:, VB, :].rearrange("p (r a d) -> p r a d", a=2, d=DH), add)
                freed(last, f"v{n}")

            def mask_row(g):
                dve.wait_ge(mask_in, g * 16 + 16)
                if not first(g):
                    full(dve, f"s{NS - 1}", g - 1)
                ts(mask[:, :, 0:L], mask_i[:, :, :], 0, MASKED, ALU.is_equal, mult).then_inc(mask_done, 1)

            def row_max(n, g):
                full(dve, f"s{n}", g)
                nc.vector.tensor_reduce(nmax[:, n, :], psum(f"s{n}")[:, :].rearrange("p (j k) -> p j k", j=4),
                                        AX.X, amax, negate=True).then_inc(nmax_done, 1)

            def reciprocals(n, g):
                taken(dve, f"s{n}", g)
                nc.vector.reciprocal(rden[:, n, :], den[:, n, :]).then_inc(rden_done, 1)

            def probs_T(n, g):
                full(dve, f"p{n}", g)
                freed(nc.vector.tensor_copy(prob_T[:, n // R, n % R, :, :],
                                            psum(f"p{n}")[:, :].rearrange("p (j q) -> p j q", j=4)), f"p{n}")

            def att_out(bp, g):
                full(dve, f"o{bp}", g)
                freed(nc.vector.tensor_copy(att_T[:, :, bp * P:(bp + 1) * P],
                                            psum(f"o{bp}")[:, 0:H * P].rearrange("p (h q) -> p h q", h=H)), f"o{bp}")

            def residual(use, dst, x, x_done, g):
                if x_done is not None:
                    dve.wait_ge(x_done, g + 1)
                full(dve, use, g)
                freed(tt(dst, psum(use)[:, :].rearrange("p (t c) -> p t c", t=TT), x, add), use)

            def rms_mean(g):
                dve.wait_ge(ss_done, g + 1)
                ts(ssm[:, :], ss[:, :], 1.0 / C, EPS0, mult, add).then_inc(ssm_done, 1)

            def rms_norm(g):
                dve.wait_ge(rms_done, g + 1)
                taken(dve, "out", g)
                for t in range(TT):
                    last = ts(nrm[:, t, :], res[:, t, :], rms[:, t:t + 1], None, mult)
                last.then_inc(nrm_done, 1)

            def norm_low(g):
                full(dve, "norm", g)
                dve.wait_ge(nhi_done, g + 1)
                for h in range(H):
                    last = stt(n_lo[:, h, :], psum("norm")[:, h * T:(h + 1) * T], cols[:, POST, h:h + 1],
                               n_hi[:, h, :].bitcast(f32), mult, sub)
                freed(last, "norm")

            def mlp_out(t, x, g):
                if t == 0:
                    dve.wait_ge(xb2_done, g + 1)
                full(dve, f"mlp{t}", g)
                freed(tt(x[:, t, :], psum(f"mlp{t}")[:, 0:C], x[:, t, :], add), f"mlp{t}")
                taken(dve, f"mlp{t}", g)
                last = nc.vector.bn_stats(stats[:, 0, t, :], x[:, t, :])
                if t == TT - 1:
                    last.then_inc(stat_done[0], 1)

            def stats_2(x, g):
                taken(dve, "wo", g)
                for t in range(TT):
                    last = nc.vector.bn_stats(stats[:, 1, t, :], x[:, t, :])
                last.then_inc(stat_done[1], 1)

            def ln_var(i, g):
                dve.wait_ge(stat_done[i], g + 1)
                nc.vector.memset(carrier[:, :], 0.0)
                for t in range(TT):
                    last = nc.vector.bn_aggr(mv[:, i, t, :], stats[:, i, t, :])
                last.then_inc(mv_done[i], 1)
                dve.wait_ge(mv_done[i], g + 1)
                ts(vare[:, i, :], mv[:, i, :, 1], EPS1, None, add).then_inc(vare_done[i], 1)

            def ln_norm(i, x, dst, g):
                dve.wait_ge(rstd_done[i], g + 1)
                for t in range(TT):
                    last = ts(dst[:, t, :], x[:, t, :], mv[:, i, t, 0:1], rstd[:, i, t:t + 1], sub, mult)
                last.then_inc(xh_done[i], 1)

            def shifted(i, use, x, d, w, bias, g):
                full(dve, use, g)
                nc.vector.tensor_copy(x[:, :, :, 0].rearrange("p h b -> p (h b)"),
                                      edge[:, bass.ds(g, 1), 1 - i, :].rearrange("p g a -> p (g a)")
                                      ).then_inc(edge_done[i], 1)
                for h in range(H):
                    last = ts(x[:, h, :, 1:L + 1], seqs(psum(use)[:, h * T:(h + 1) * T]), cols[:, w, h:h + 1],
                              cols[:, bias, h:h + 1], mult, add)
                freed(last, use)
                dve.wait_ge(edge_done[i], g + 1)
                taken(dve, use, g)
                tt(d[:, :, :, :].rearrange("p h b l -> p (h b) l"),
                   x[:, :, :, 0:L].rearrange("p h b l -> p (h b) l"),
                   x[:, :, :, 1:L + 1].rearrange("p h b l -> p (h b) l"), sub).then_inc(sx_done[i], 1)
                dve.wait_ge(sx_done[i], g + 1)

            def lerp(dst, x, d, col, h):
                return stt(seqs(dst[:, h, :]), d[:, h, :, :], cols[:, col, h:h + 1], x[:, h, :, 1:L + 1], mult, add)

            def maa_in(g):
                for h in range(H):
                    last = lerp(xx, xa, sx, MAAX, h)
                last.then_inc(xx_done, 1)

            def mix_m(f, g):
                full(dve, f"mix{f}", g)
                for h in range(H):
                    last = stt(mixed[f][:, h, :], psum(f"mix{f}")[:, h * T:(h + 1) * T], cols[:, MAA0 + f, h:h + 1],
                               sx[:, h, :, :].rearrange("p b l -> p (b l)"), add, mult)
                freed(last, f"mix{f}")

            def v_low(g):
                dve.wait_ge(vhi_done, g + 1)
                freed(tt(v_lo[:, :], psum("v")[:, :], v_hi[:, :].bitcast(f32), sub), "v")

            def gate_out(g):
                dve.wait_ge(tg_done, g + 1)
                freed(stt(gate[:, :, :].rearrange("p h t -> p (h t)"), gate[:, :, :].rearrange("p h t -> p (h t)"),
                          1.0, psum("g")[:, :], add, mult), "g")

            def r_u_k(g):
                taken(dve, "r", g)
                for h in range(H):
                    last = stt(ruk[:, h, :], k1[:, h, :, :].rearrange("p b l -> p (b l)"), cols[:, U, h:h + 1],
                               r1[:, h, :, :].rearrange("p b l -> p (b l)"), mult, mult)
                last.then_inc(ruk_done, 1)

            def bonus_out(g):
                taken(dve, "vc", g)
                full(dve, "bonus", g)
                freed(tt(bonus[:, :], psum("bonus")[:, :], v_c[:, :], mult), "bonus")

            def scan(t, g):
                full(dve, f"vr{t}", g)
                if t == 0:
                    dve.wait_ge(w_done, g + 1)
                    dve.wait_ge(s0_done, g + 1)
                freed(tt(kv[:, t, :, 1:L], k1[:, :, :, 0:L - 1].rearrange("p h b l -> p (h b) l"),
                         psum(f"vr{t}")[:, :].rearrange("p (a l) -> p a l", l=L)[:, :, 0:L - 1], mult), f"vr{t}")
                taken(dve, f"vr{t}", g)
                states = kv[:, t, :, :].rearrange("p a l -> p (a l)")
                nc.vector.tensor_tensor_scan(states, w_sh[:, :, :, :].rearrange("p h b l -> p (h b l)"), states,
                                             0.0, mult, add).then_inc(state_done, 1)

            def y_out(g):
                full(dve, "yc", g)
                taken(dve, "bonus", g)
                freed(tt(yc[:, :, :].rearrange("p h t -> p (h t)"), psum("yc")[:, :], bonus[:, :], add), "yc")

            def var_out(g):
                full(dve, "var", g)
                freed(ts(gv[:, :], psum("var")[:, 0:TT * NH1], EPS1, None, add), "var")

            def widen(g):
                taken(dve, "var", g)
                ts(g_rstd[:, :].bitcast(i32), gv[:, :].bitcast(i32), -0.5, float(0x5f3759df), mult,
                   add).then_inc(newton_done, 1)
                for n in range(3):
                    k = g * 10 + 3 * n
                    dve.wait_ge(newton_done, k + 1)
                    tt(g_t[:, :], g_rstd[:, :], g_rstd[:, :], mult).then_inc(newton_done, 1)
                    dve.wait_ge(newton_done, k + 2)
                    stt(g_t[:, :], g_t[:, :], -0.5, gv[:, :], mult, mult).then_inc(newton_done, 1)
                    dve.wait_ge(newton_done, k + 3)
                    stt(g_rstd[:, :], g_t[:, :], 1.5, g_rstd[:, :], add, mult).then_inc(newton_done, 1)
                dve.wait_ge(newton_done, g * 10 + 10)
                nc.vector.tensor_copy(g_wide.rearrange("p t (n s) -> p (t n) s", s=S),
                                      g_rstd[:, :].unsqueeze(2).broadcast_to([P, TT * NH1, S])
                                      ).then_inc(gwide_done, 1)

            def group_norm(g):
                full(dve, "rstd", g)
                freed(tt(z[:, :, :].rearrange("p h t -> p (h t)"), psum("rstd")[:, :],
                         yc[:, :, :].rearrange("p h t -> p (h t)"), mult), "rstd")

            def gated(g):
                taken(dve, "rstd", g)
                for h in range(H):
                    last = ts(z[:, h, :], z[:, h, :], gn_half[:, 0, h:h + 1], gn_half[:, 1, h:h + 1], mult, add)
                last.then_inc(z2_done, 1)
                dve.wait_ge(z2_done, g + 1)
                taken(dve, "g", g)
                tt(z[:, :, :], z[:, :, :], gate[:, :, :], mult).then_inc(z_done, 1)

            def ffn_in(g):
                for dst, col in ((xk2, FMK), (xr2, FMR)):
                    for h in range(H):
                        last = lerp(dst, xc, sc, col, h)
                last.then_inc(xkr_done, 1)

            def value_gated(g):
                full(dve, "fv", g)
                taken(dve, "fr", g)
                freed(stt(tr[:, :, :].rearrange("p t c -> p (t c)"), tr[:, :, :].rearrange("p t c -> p (t c)"), 1.0,
                          psum("fv")[:, :], add, mult), "fv")

            def out(g):
                if not first(g):
                    dve.wait_ge(out_done, g * 16)
                taken(dve, "fv", g)
                stt(o[:, :, :], tr[:, :, :], 0.5, x2[:, :, :], mult, add).then_inc(o_done, 1)

            def w1_low():
                dve.wait_ge(w1_hi_done, 1)
                for x, k, m in w1_parts:
                    part = (slice(None), k, slice(m * 2 * T, (m + 1) * 2 * T))
                    last = tt(w1_lo[part], x[:, :, :].rearrange("p h t -> p (h t)"), w1_hi[part].bitcast(f32), sub)
                last.then_inc(w1_split, 1)

            def both(g0, g1, g2, par):
                a, b, c = (g is not None for g in (g0, g1, g2))
                if a: mask_row(g0)
                if b:
                    shifted(0, "xa", xa, sx, LN1W, LN1B, g1)
                    maa_in(g1)
                if c: group_norm(g2)
                if a: v_out(0, g0)
                for n in range(NS + 3):
                    if a and n < NS: row_max(n, g0)
                    if a and 1 <= n <= NS: reciprocals(n - 1, g0)
                    if c and n == 7: ffn_in(g2)
                    if b and n == 3: v_low(g1)
                    if b and n < MAA: mix_m(MIX_ORDER[n], g1)
                    if c and n == 0: gated(g2)
                    if a and n == 0: v_out(1, g0)
                    if c and n == 1:
                        if not first(g2):
                            dve.wait_ge(o_done, g2)
                        residual("wo", x2[:, :, :], x1[:, par, :, :], None, g2)
                    if c and n == 2: stats_2(x2, g2); ln_var(1, g2)
                    if c and n == 3: ln_norm(1, x2, xh2, g2)
                    if b and n == 6: r_u_k(g1)
                    if a and n == 8:
                        att_out(0, g0)
                    if a and n >= 3 and n % 2 == 0: probs_T(n - 3, g0)
                    if c and n == 5: shifted(1, "xc", xc, sc, LN2W, LN2B, g2)
                    if b and n == 8: bonus_out(g1)
                    if b and n == 9: scan(0, g1)
                if b: scan(1, g1)
                if a: att_out(1, g0)
                if b: scan(2, g1)
                if a: residual("out", res, x_ob[:, :, :], xob_done, g0)
                if b: scan(3, g1)
                if a: rms_mean(g0)
                if b: scan(4, g1)
                if a:
                    rms_norm(g0)
                    if first(g0): w1_low()
                if c: value_gated(g2)
                if b: scan(5, g1)
                if a: norm_low(g0)
                if b: gate_out(g1)
                if b: scan(6, g1); scan(7, g1)
                if c: out(g2)
                if b:
                    y_out(g1)
                if a: mlp_out(0, x1[:, par, :, :], g0)
                if b: var_out(g1); widen(g1)
                if a: mlp_out(1, x1[:, par, :, :], g0); ln_var(0, g0); ln_norm(0, x1[:, par, :, :], xh, g0)

            nc.vector.memset(w_sh[:, :, :, 0], 0.0).then_inc(setup, 1)
            nc.vector.memset(v_z[:, :, :, :, :], 0.0).then_inc(setup, 1)
            nc.vector.memset(mask[:, :, L:KEYS], 0.0).then_inc(setup, 1)
            nc.vector.memset(ones[:, :], 1.0).then_inc(setup, 1)
            nc.vector.memset(power[:, :], -0.5).then_inc(setup, 1)
            dve.wait_ge(small_w, 16 * len(SMALL))
            ts(gn_half[:, :, :], cols[:, GNW:GNB + 1, :], 0.5, None, mult).then_inc(setup, 1)
            for par in range(2):
                last = ts(q_bias[:, :, par], cols[:, QB, :], parity[:, par:par + 1], None, mult)
            last.then_inc(setup, 1)
            for i in range(3):
                dve.wait_ge(qkv_hi_done, i + 1)
                tt(qkv_lo[:, i, :, :].rearrange("p h c -> p (h c)"), qkv_w[i],
                   qkv_hi[:, i, :, :].rearrange("p h c -> p (h c)").bitcast(f32), sub).then_inc(qkv_lo_done, 1)
            dve.wait_ge(setup, SETUP)
            both(0, None, None, 0)
            dve.wait_ge(l1_w, 16 * len(L1_LOADS))
            nc.vector.tensor_copy(rep[:, :, :], kv[:, 0:2, :, :].rearrange("p s a l -> p (s a l)")
                                  .rearrange("p (t m) -> p t m", t=S)).then_inc(l1_const, 1)
            nc.vector.tensor_copy(centre[:, :], kv[:, 2, 0:2, :].rearrange("p a l -> p (a l)")).then_inc(l1_const, 1)
            for w, hi in ((wg_in, wg_hi), (fwr_in, fwr_hi)):
                last = nc.vector.tensor_copy(hi[:, :, :], w)
            last.then_inc(w_hi_done, 1)
            dve.wait_ge(w_hi_done, 1)
            for w, hi, lo in ((wg_in, wg_hi, wg_lo), (fwr_in, fwr_hi, fwr_lo)):
                tt(lo[:, :, :], w, hi[:, :, :].bitcast(f32), sub).then_inc(l1_const, 1)
            both(1, 0, None, 1)
            with dve.Fori(2, GROUPS - 2, 2) as i:
                both(i, i - 1, i - 2, 0)
                both(i + 1, i, i - 1, 1)
            both(GROUPS - 2, GROUPS - 3, GROUPS - 4, 0)
            both(GROUPS - 1, GROUPS - 2, GROUPS - 3, 1)
            both(None, GROUPS - 1, GROUPS - 2, 0)
            both(None, None, GROUPS - 1, 1)


def shape_constants():
    p = np.arange(P)
    same = (p[:, None] // S == p[None, :] // S).astype(np.float32)
    at = (p[None, :] % S == np.arange(S)[:, None]).astype(np.float32)
    t, n = p // 32 + 4 * (p % 32 // 16), p % 16
    to_heads = ((n[:, None] == p[None, :] // S) * ((t[:, None] == p[None, :] % S) - 1 / S)).astype(np.float32)
    return {
        "ident": np.eye(P, dtype=np.float32),
        "block": same,
        "centre": np.eye(P, dtype=np.float32) - same / S,
        "mean16": np.ascontiguousarray((p[:, None] // S == np.arange(P // S)[None, :]).astype(np.float32) / S),
        "rep": np.ascontiguousarray((same[:, None, :] * at.T[:, :, None]).astype(np.float32)),
        "head_sum": np.stack([(p[:, None] // S == np.arange(32)[None, :] - 16 * i).astype(np.float32)
                              for i in range(2)], axis=1),
        "to_heads": to_heads,
        "parity": np.stack([(p // DH % 2 == i).astype(np.float32) / DH for i in range(2)], axis=1),
    }


def kernel(**inputs):
    import concourse.bacc as bacc
    from concourse.bass_utils import run_bass_kernel_spmd

    a = {k: np.asarray(v) for k, v in inputs.items()}
    l0 = {k[len("L0_xattn_"):]: v for k, v in a.items() if k.startswith("L0_xattn_")}
    l1 = {k[len("L1_xattn_"):]: v for k, v in a.items() if k.startswith("L1_xattn_")}

    def rows_of(w):
        return np.ascontiguousarray(w.reshape(-1, P, w.shape[1]).transpose(1, 0, 2))

    def half_cols(v):
        return np.ascontiguousarray(v.reshape(-1, H, P).transpose(2, 0, 1))

    x, ctx = a["x"], a["ctx_2048"]
    h = np.concatenate([ctx, x], axis=1)
    h_T = h.reshape(GROUPS, GB, KEYS, H, P).transpose(0, 4, 3, 1, 2)
    vectors = [l0["q_b"], l0["kv_b"][0::2], l0["postnorm_w"], l1["ln1_w"], l1["ln1_b"], l1["ln2_w"], l1["ln2_b"],
               l1["maa_x"], l1["maa_w"], l1["maa_k"], l1["maa_v"], l1["maa_r"], l1["maa_g"], l1["time_decay"],
               l1["faaaa"].reshape(C), l1["gn_w"], l1["gn_b"], l1["fmaa_k"], l1["fmaa_r"]]
    s0 = ctx[:, 2:2 + S, :].reshape(GROUPS, GB, H, P, S).transpose(3, 0, 4, 2, 1)
    edge = ctx[:, 0:2, :].reshape(GROUPS, GB, 2, H, P).transpose(4, 0, 2, 3, 1)
    arrays = {
        "x": np.ascontiguousarray(x.reshape(B * L, C)),
        "h_T": np.ascontiguousarray(h_T).reshape(GROUPS, P, H * GB * KEYS),
        "q_w": rows_of(l0["q_w"]), "k_w": rows_of(l0["kv_w"][:, 0::2]), "v_w": rows_of(l0["kv_w"][:, 1::2]),
        "out_w": rows_of(l0["out_w"]), "w1": rows_of(l0["mlp_w1"]), "w2": rows_of(l0["mlp_w2"]),
        "b1": np.ascontiguousarray(l0["mlp_b1"].reshape(FC, P).T),
        "rows": np.ascontiguousarray(np.broadcast_to(
            np.stack([l0["kv_b"][1::2], l0["out_b"], l0["mlp_b2"]])[None], (P, 3, C))),
        "cols": half_cols(np.stack(vectors)),
        "mask": np.ascontiguousarray(a["mask_BxS2_ik0"]).reshape(1, B, L),
        "maa_w1": rows_of(l1["maa_w1"]),
        "maa_w2": np.ascontiguousarray(l1["maa_w2"][0:4].reshape(P, C)),
        "maa_w2g": np.ascontiguousarray(l1["maa_w2"][4]),
        "decay_w1": rows_of(l1["decay_w1"]), "decay_w2": l1["decay_w2"],
        "wr": rows_of(l1["Wr"].T), "wk": rows_of(l1["Wk"].T), "wv": rows_of(l1["Wv"].T), "wg": rows_of(l1["Wg"].T),
        "wo": rows_of(l1["Wo"].T), "fwk": rows_of(l1["fWk"].T), "fwr": rows_of(l1["fWr"].T),
        "fwv": rows_of(l1["fWv"].T),
        "s0": np.ascontiguousarray(s0).reshape(P, GROUPS, S, H * GB),
        "edge": np.ascontiguousarray(edge).reshape(P, GROUPS, 2, H * GB),
        **shape_constants(),
    }
    nc = bacc.Bacc("TRN2", target_bir_lowering=False, num_devices=1)
    io = {n: nc.dram_tensor(f"in_{n}", v.shape, mybir.dt.from_np(v.dtype), kind="ExternalInput").ap()
          for n, v in arrays.items()}
    io["out"] = nc.dram_tensor("out", (B * L, C), mybir.dt.float32, kind="ExternalOutput").ap()
    build(nc, io)
    r = run_bass_kernel_spmd(nc, [{f"in_{n}": v for n, v in arrays.items()}], core_ids=[0])
    return r.results[0]["out"].reshape(B, L, C)
```
